# Optimizing a Trainium2 kernel written in Bass

```python
import numpy as np
import jax
import jax.numpy as jnp

def _softmax(x, axis=-1):
    return jax.nn.softmax(x, axis=axis)

def _gelu(x):
    return jax.nn.gelu(x, approximate=True)

def _silu(x):
    return jax.nn.silu(x)

def _sigmoid(x):
    return jax.nn.sigmoid(x)

def _layernorm(x, axis=-1, eps=1e-05):
    m = jnp.mean(x, axis=axis, keepdims=True)
    v = jnp.var(x, axis=axis, keepdims=True)
    return (x - m) / jnp.sqrt(v + eps)

def _scatter_add(tgt, idx, src, axis=0):
    return tgt.at[idx].add(src)

def _segment_sum(src, seg, n):
    return jax.ops.segment_sum(src, seg, n)
kernel_name = 'mk_sandwich_d1_jaxref_r8_afa092'

def setup_inputs(seed: int=0):
    np.random.seed(seed)
    _w = jnp.asarray

    def _L0_attn_setup():
        import jax, jax.numpy as jnp
        import numpy as np
        B, S, E, H = (4, 512, 128, 16)
        D = E // H

        def _phi(x):
            return jax.nn.elu(x) + 1.0
        key = jax.random.key(seed)
        k1, k2, k3 = jax.random.split(key, 3)
        x = jax.random.normal(k1, (B, S, E), dtype=jnp.float32)
        W_qkv = jax.random.normal(k2, (E, 3 * E), dtype=jnp.float32) * E ** (-0.5)
        b_qkv = jnp.zeros((3 * E,), dtype=jnp.float32)
        W_proj = jax.random.normal(k3, (E, E), dtype=jnp.float32) * E ** (-0.5)
        b_proj = jnp.zeros((E,), dtype=jnp.float32)
        return {'x': x, 'W_qkv': W_qkv, 'b_qkv': b_qkv, 'W_proj': W_proj, 'b_proj': b_proj}
    _L0_attn_in = _L0_attn_setup()

    def _L0_ffn_setup():
        import jax, jax.numpy as jnp
        import numpy as np
        EPS = 1e-05
        LN_EPS = 1e-05
        NUM_EXPERTS = 8
        TOP_K = 2
        HIDDEN = 128
        INTER = 256

        def _swiglu(x, wg, wu, wd):
            return jax.nn.silu(x @ wg) * (x @ wu) @ wd
        key = jax.random.key(seed)
        ks = jax.random.split(key, 10)
        B, S, H, I, E = (8, 512, HIDDEN, INTER, NUM_EXPERTS)
        std_h = 1.0 / np.sqrt(H)
        std_i = 1.0 / np.sqrt(I)
        return {'x': jax.random.normal(ks[0], (B, S, H), dtype=jnp.float32), 'ln_scale': jnp.ones((H,), dtype=jnp.float32), 'ln_bias': jnp.zeros((H,), dtype=jnp.float32), 'gate_w': jax.random.normal(ks[1], (E, H), dtype=jnp.float32) * 0.01, 'Wg': jax.random.normal(ks[2], (E, H, I), dtype=jnp.float32) * std_h, 'Wu': jax.random.normal(ks[3], (E, H, I), dtype=jnp.float32) * std_h, 'Wd': jax.random.normal(ks[4], (E, I, H), dtype=jnp.float32) * std_i, 'sWg': jax.random.normal(ks[5], (H, I), dtype=jnp.float32) * std_h, 'sWu': jax.random.normal(ks[6], (H, I), dtype=jnp.float32) * std_h, 'sWd': jax.random.normal(ks[7], (I, H), dtype=jnp.float32) * std_i}
    _L0_ffn_in = _L0_ffn_setup()
    _d = {'L0_attn_x': _L0_attn_in['x'], 'L0_attn_W_qkv': _L0_attn_in['W_qkv'], 'L0_attn_b_qkv': _L0_attn_in['b_qkv'], 'L0_attn_W_proj': _L0_attn_in['W_proj'], 'L0_attn_b_proj': _L0_attn_in['b_proj'], 'L0_ffn_ln_scale': _L0_ffn_in['ln_scale'], 'L0_ffn_ln_bias': _L0_ffn_in['ln_bias'], 'L0_ffn_gate_w': _L0_ffn_in['gate_w'], 'L0_ffn_Wg': _L0_ffn_in['Wg'], 'L0_ffn_Wu': _L0_ffn_in['Wu'], 'L0_ffn_Wd': _L0_ffn_in['Wd'], 'L0_ffn_sWg': _L0_ffn_in['sWg'], 'L0_ffn_sWu': _L0_ffn_in['sWu'], 'L0_ffn_sWd': _L0_ffn_in['sWd']}
    _x0 = _d['L0_attn_x']
    _d['L0_attn_x'] = jax.random.normal(jax.random.fold_in(jax.random.key(seed), 1), (8, 1024, 128), dtype=_x0.dtype)
    del _x0
    return _d

def reference(L0_attn_x, L0_attn_W_qkv, L0_attn_b_qkv, L0_attn_W_proj, L0_attn_b_proj, L0_ffn_ln_scale, L0_ffn_ln_bias, L0_ffn_gate_w, L0_ffn_Wg, L0_ffn_Wu, L0_ffn_Wd, L0_ffn_sWg, L0_ffn_sWu, L0_ffn_sWd):

    def _L0_attn_ref(x, W_qkv, b_qkv, W_proj, b_proj):
        import jax, jax.numpy as jnp
        import numpy as np
        B, S, E, H = (4, 512, 128, 16)
        D = E // H

        def _phi(x):
            return jax.nn.elu(x) + 1.0
        b, s, _ = x.shape
        qkv = (x @ W_qkv + b_qkv).reshape(b, s, 3, H, D)
        q, k, v = (qkv[:, :, 0], qkv[:, :, 1], qkv[:, :, 2])
        pq, pk = (_phi(q), _phi(k))
        kv = jnp.einsum('bshd,bshm->bhmd', pk, v)
        z = 1.0 / (jnp.einsum('bshd,bhd->bsh', pq, pk.sum(axis=1)) + 1e-06)
        attn = jnp.einsum('bshd,bhmd,bsh->bshm', pq, kv, z)
        attn = attn.reshape(b, s, H * D)
        _proj = attn @ W_proj + b_proj
        return attn

    def _L0_ffn_ref(x, ln_scale, ln_bias, gate_w, Wg, Wu, Wd, sWg, sWu, sWd):
        import jax, jax.numpy as jnp
        import numpy as np
        EPS = 1e-05
        LN_EPS = 1e-05
        NUM_EXPERTS = 8
        TOP_K = 2
        HIDDEN = 128
        INTER = 256

        def _swiglu(x, wg, wu, wd):
            return jax.nn.silu(x @ wg) * (x @ wu) @ wd
        B, S, H = x.shape
        xf = x.reshape(-1, H)
        mu = jnp.mean(xf, axis=-1, keepdims=True)
        var = jnp.var(xf, axis=-1, keepdims=True)
        xn = (xf - mu) * jax.lax.rsqrt(var + LN_EPS) * ln_scale + ln_bias
        logits = xn @ gate_w.T
        probs = jax.nn.softmax(logits, axis=-1)
        tk_probs, tk_idx = jax.lax.top_k(probs, TOP_K)
        tk_probs = tk_probs / (jnp.sum(tk_probs, axis=-1, keepdims=True) + EPS)
        onehot = tk_idx[..., None] == jnp.arange(NUM_EXPERTS)[None, None, :]
        w = jnp.sum(tk_probs[..., None] * onehot.astype(tk_probs.dtype), axis=1)
        out = _swiglu(xf, sWg, sWu, sWd)
        for e in range(NUM_EXPERTS):
            out = out + w[:, e:e + 1] * _swiglu(xf, Wg[e], Wu[e], Wd[e])
        return out.reshape(B, S, H)
    x = L0_attn_x
    x = x + _layernorm(_L0_attn_ref(_layernorm(x, axis=-1), L0_attn_W_qkv, L0_attn_b_qkv, L0_attn_W_proj, L0_attn_b_proj), axis=-1)
    x = x + _layernorm(_L0_ffn_ref(_layernorm(x, axis=-1), L0_ffn_ln_scale, L0_ffn_ln_bias, L0_ffn_gate_w, L0_ffn_Wg, L0_ffn_Wu, L0_ffn_Wd, L0_ffn_sWg, L0_ffn_sWu, L0_ffn_sWd), axis=-1)
    return x

_drawn_inputs = setup_inputs


def setup_inputs(seed=0):
    import zlib

    import numpy as np

    out = dict(_drawn_inputs(seed))
    spreads = {'L0_attn_b_qkv': (0.0, 0.1),
     'L0_attn_b_proj': (0.0, 0.1),
     'L0_ffn_ln_scale': (1.0, 0.2),
     'L0_ffn_ln_bias': (0.0, 0.1)}
    factors = {}
    for name, (base, spread) in spreads.items():
        noise = np.random.default_rng([zlib.crc32(name.encode()), seed]).standard_normal(out[name].shape)
        drawn = base * np.exp(spread * noise) if base else spread * noise
        out[name] = jnp.asarray(drawn.astype(out[name].dtype))
    for name, factor in factors.items():
        out[name] = (out[name] * factor).astype(out[name].dtype)
    return out
```

```python
import concourse.bass as bass
from concourse import mybir
from contextlib import ExitStack

P = 128
E = 128
B, S = 8, 1024
NT = S // P
HEADS, D = 16, 8
INTER = 256
IC = INTER // P
NE = 8
TOK = B * S
CAP = TOK + P
ROW = E + 2
UNITS = 2 * TOK // P + NE
SLOTS = NE * CAP + NE * P
PADS = 2 * (NE * P + NE * P)
QU = 4
LN_EPS = 1e-5
EPS = 1e-5
SHIFT = 17
DVE_PAIR = 152
DVE_C = 32
KEEP = 2 * NT * E + 3 * NT


def program(nc, x, w_qkv, b_qkv, w_proj, b_proj, ln_scale, ln_bias, gate_w, wg, wu, wd, swg, swu, swd, out):
    f32, bf16, i32 = mybir.dt.float32, mybir.dt.bfloat16, mybir.dt.int32
    ALU, ACT, AX = mybir.AluOpType, mybir.ActivationFunctionType, mybir.AxisListType
    ds = bass.ds

    x_v = x.rearrange("b (p t) f -> b p (t f)", t=NT)
    out_v = out.rearrange("b (p t) f -> b p (t f)", t=NT)
    slots_dram = nc.dram_tensor("slots_dram", (SLOTS, ROW), f32, kind="Internal").ap()
    routed_dram = nc.dram_tensor("routed_dram", (2 * TOK + PADS, E), f32, kind="Internal").ap()
    routed_v = routed_dram[0:2 * TOK, :].rearrange("(b p t) f -> b p (t f)", b=B, p=P)
    keep_dram = nc.dram_tensor("keep_dram", (B, P, KEEP), f32, kind="Internal").ap()

    ctx = ExitStack()
    with ctx:
        def sb(name, shape, dt=f32):
            return ctx.enter_context(nc.sbuf_tensor(name, shape, dt))

        def pb(name):
            return ctx.enter_context(nc.psum_tensor(name, [P, 512], f32))

        def sem(name):
            return ctx.enter_context(nc.semaphore(name))

        wqkv = sb("wqkv", [P, 3 * E])
        wgu = sb("wgu", [P, NE, 2 * INTER])
        wdn = sb("wdn", [P, NE, IC * E])
        swgu = sb("swgu", [P, 2 * INTER])
        swdn = sb("swdn", [P, IC * E])
        ident = sb("ident", [P, P])
        ones = sb("ones", [P, P])
        ones_bf = sb("ones_bf", [P, 512], bf16)
        tri = sb("tri", [P, P], bf16)
        head_mask = sb("head_mask", [P, HEADS])
        bias3 = sb("bias3", [P, 3 * E])
        bias_bf = sb("bias_bf", [P, 3 * E], bf16)
        bias_part = sb("bias_part", [P, 3 * E], bf16)
        bias_acc = sb("bias_acc", [P, 3 * E])
        gate_t = sb("gate_t", [P, NE])
        gate_s = sb("gate_s", [P, NE])
        gate_c = sb("gate_c", [P, NE])
        gate_b = sb("gate_b", [P, NE])
        ln_sc = sb("ln_sc", [P, 1])
        ln_bi = sb("ln_bi", [P, 1])
        ln_bi_w = sb("ln_bi_w", [P, P])
        minus1 = sb("minus1", [P, 1])
        rank_of = sb("rank_of", [P, NE])
        region = sb("region", [P, NE])
        tok2 = sb("tok2", [P, B * NT])
        lower8 = sb("lower8", [P, NE, NE])
        unit_no = sb("unit_no", [P, UNITS])
        pad_rows = sb("pad_rows", [P, NE, ROW])
        spare_rows = sb("spare_rows", [P, NE, ROW])
        part_no = sb("part_no", [P, NE])

        xin = [sb(f"xin{i}", [P, NT, E]) for i in range(2)]
        keep = [sb(f"keep{i}", [P, KEEP]) for i in range(2)]
        u_row = [sb(f"u_row{i}", [P, NT, ROW]) for i in range(2)]
        slot_i = [sb(f"slot_i{i}", [P, 2 * NT], i32) for i in range(2)]
        xn = sb("xn", [P, NT, E])
        xnT = sb("xnT", [P, S])
        q_e = sb("q_e", [P, 2, 512])
        k_e = sb("k_e", [P, 2, 2, E])
        pqT = sb("pqT", [P, S])
        pk = sb("pk", [P, NT, E])
        v1 = sb("v1", [P, NT, E + 1])
        kvm = sb("kvm", [P, E + HEADS])
        att = sb("att", [P, NT, E])
        zt = sb("zt", [P, 2, 2, HEADS])
        zr = sb("zr", [P, 2, 2, HEADS])
        uT = sb("uT", [P, S])
        st_a = sb("st_a", [P, NT, 6])
        st_1 = sb("st_1", [P, NT, 6])
        mv_a = sb("mv_a", [P, NT, 2])
        mv_u = sb("mv_u", [P, NT, 2])
        mv_1 = sb("mv_1", [P, NT, 2])
        ve = sb("ve", [P, 2 * NT])
        rs = sb("rs", [P, 2 * NT])
        nt_ = sb("nt_", [P, 2 * NT])
        r_a = sb("r_a", [P, NT])
        r_u = sb("r_u", [P, NT])
        r_41 = sb("r_41", [P, 2 * NT])
        lg = sb("lg", [P, NT, NE])
        lg2 = sb("lg2", [P, NT, NE])
        cand = sb("cand", [P, NT, NE])
        oh1 = sb("oh1", [P, NT, NE])
        oh2 = sb("oh2", [P, NT, NE])
        oh_bf = sb("oh_bf", [P, NT, NE], bf16)
        total = sb("total", [P, NE])
        total_new = sb("total_new", [P, NE])
        total_bf = sb("total_bf", [P, NE], bf16)
        m1 = sb("m1", [P, NT])
        m2 = sb("m2", [P, NT])
        i1 = sb("i1", [P, NT])
        i2 = sb("i2", [P, NT])
        r_in = sb("r_in", [P, NT, NE + 1])
        r_exp = sb("r_exp", [P, NT, NE + 1])
        esum = sb("esum", [P, NT])
        den = sb("den", [P, NT])
        wden = sb("wden", [P, NT])
        pos = sb("pos", [P, NT, NE])
        slot_f = sb("slot_f", [P, 2 * NT])
        act_g = sb("act_g", [P, 2, INTER])
        hid = sb("hid", [P, 2, INTER])
        hidT = sb("hidT", [P, 2, INTER])
        xb = [sb(f"xb{i}", [P, ROW]) for i in range(QU)]
        xbT = sb("xbT", [P, 2, P])
        yb = [sb(f"yb{i}", [P, E]) for i in range(QU)]
        yi = [sb(f"yi{i}", [P, 1], i32) for i in range(QU)]
        cnt = sb("cnt", [P, NE])
        tl_i = sb("tl_i", [P, NE], i32)
        tl_s = sb("tl_s", [P, NE], i32)
        tl = sb("tl", [P, NE])
        tl8 = sb("tl8", [P, NE, NE])
        cum = sb("cum", [P, NE])
        gain = sb("gain", [P, NE])
        past = sb("past", [P, UNITS, NE])
        pk_sum = sb("pk_sum", [P, UNITS])
        pk_i = sb("pk_i", [P, UNITS], i32)
        unit_row = sb("unit_row", [P, UNITS], i32)
        unit_e = sb("unit_e", [P, UNITS], i32)
        unit_ef = sb("unit_ef", [P, UNITS])
        unit_w = sb("unit_w", [P, UNITS], i32)
        pad_f = sb("pad_f", [P, NE])
        pad_i = sb("pad_i", [P, NE], i32)
        yin = [sb(f"yin{i}", [P, NT, 2, E]) for i in range(2)]
        res = [sb(f"res{i}", [P, NT, E]) for i in range(2)]
        shift = sb("shift", [P, NT])

        bank_t = [pb("bank_t0"), pb("bank_t1")]
        bank_p = [pb("bank_p0"), pb("bank_p1")]
        bank_g = [pb("bank_g0"), pb("bank_g1")]
        bank_h = [pb("bank_h0"), pb("bank_h1")]

        w_loaded, sw_loaded, ew_loaded = sem("w_loaded"), sem("sw_loaded"), sem("ew_loaded")
        x_loaded = [sem("x_loaded0"), sem("x_loaded1")]
        consts = sem("consts")
        spare_in = sem("spare_in")
        setup = sem("setup")
        setup_ps = sem("setup_ps")
        attn_ps, xnT_ps, q_ps, kv_ps, sum_ps = sem("attn_ps"), sem("xnT_ps"), sem("q_ps"), sem("kv_ps"), sem("sum_ps")
        uT_ps, logit_ps, rank_ps = sem("uT_ps"), sem("logit_ps"), sem("rank_ps")
        gu_ps, ht_ps, y_ps, xbT_ps = sem("gu_ps"), sem("ht_ps"), sem("y_ps"), sem("xbT_ps")
        cnt_ps = sem("cnt_ps")
        xnT_sb, q_exp, kv_exp, uT_sb, r_done = sem("xnT_sb"), sem("q_exp"), sem("kv_exp"), sem("uT_sb"), sem("r_done")
        silu, ht_sb, y_sb = sem("silu"), sem("ht_sb"), sem("y_sb")
        out_add = sem("out_add")
        dve = sem("dve")
        dve_passed, pool_passed = sem("dve_passed"), sem("pool_passed")
        att_sb, pq_sb, pk_sb, kvm_sb, xn_sb, u_sb = sem("att_sb"), sem("pq_sb"), sem("pk_sb"), sem("kvm_sb"), sem("xn_sb"), sem("u_sb")
        x1_done = sem("x1_done")
        r_ready, oh_ready, slots_ready, keep_ready = sem("r_ready"), sem("oh_ready"), sem("slots_ready"), sem("keep_ready")
        hid_sb, xbT_sb, yi_sb = sem("hid_sb"), sem("xbT_sb"), sem("yi_sb")
        pads_ready, table_ready = sem("pads_ready"), sem("table_ready")
        res_ready = sem("res_ready")
        scattered = [sem("scattered0"), sem("scattered1")]
        kept = [sem("kept0"), sem("kept1")]
        pads_in = sem("pads_in")
        xb_in = [sem(f"xb_in{i}") for i in range(QU)]
        y_out = [sem(f"y_out{i}") for i in range(QU)]
        c_in = [sem("c_in0"), sem("c_in1")]
        stored = [sem("stored0"), sem("stored1")]

        def of(b, n, k=0):
            return b * n + k

        def is_int(b):
            return isinstance(b, int)

        def schedule(eng, step, back):
            step(1, 1)
            step(2, 0)
            with eng.Fori(0, (B - 4) // 2) as j:
                step(j * 2 + 3, 1)
                step(j * 2 + 4, 0)
            step(B - 1, 1)
            back(B - 1, 1)

        block = ctx.enter_context(nc.Block())

        @block.sync
        def _(sp):
            sp.dma_start(xin[0][:, :, :], x_v[0, :, :]).then_inc(x_loaded[0], 16)
            sp.dma_start(wqkv[:, :], w_qkv).then_inc(w_loaded, 16)
            for i in range(3):
                sp.dma_start(bias3[i:i + 1, :], b_qkv.rearrange("(a n) -> a n", a=1)).then_inc(w_loaded, 16)
            sp.dma_start(gate_t[:, :], gate_w.rearrange("e f -> f e"), allow_slow_non_contiguous=True).then_inc(w_loaded, 16)
            sp.dma_start(ln_sc[:, :], ln_scale.rearrange("(f a) -> f a", a=1)).then_inc(w_loaded, 16)
            sp.dma_start(ln_bi[:, :], ln_bias.rearrange("(f a) -> f a", a=1)).then_inc(w_loaded, 16)
            sp.dma_start(xin[1][:, :, :], x_v[1, :, :]).then_inc(x_loaded[1], 16)
            sp.dma_start(swgu[:, 0:INTER], swg).then_inc(sw_loaded, 16)
            sp.dma_start(swgu[:, INTER:2 * INTER], swu).then_inc(sw_loaded, 16)
            sp.dma_start(swdn[:, :].rearrange("p (c n) -> p c n", c=IC), swd.rearrange("(c p) n -> p c n", p=P)).then_inc(sw_loaded, 16)
            sp.dma_start(wgu[:, :, 0:INTER], wg.rearrange("e p n -> p e n")).then_inc(ew_loaded, 16)
            sp.dma_start(wgu[:, :, INTER:2 * INTER], wu.rearrange("e p n -> p e n")).then_inc(ew_loaded, 16)
            for e in range(NE):
                sp.dma_start(wdn[:, e, :].rearrange("p (c n) -> p c n", c=IC), wd[e, :, :].rearrange("(c p) n -> p c n", p=P)).then_inc(ew_loaded, 16)
            sp.wait_ge(consts, 1)
            sp.dma_start(slots_dram[NE * CAP:SLOTS, :].rearrange("(p e) n -> p (e n)", p=P),
                         spare_rows[:, :, :].rearrange("p e n -> p (e n)")).then_inc(spare_in, 16)

            def store(k, par):
                sp.wait_ge(keep_ready, of(k, 1, 1))
                sp.wait_ge(y_sb, of(k, NT, NT))
                sp.dma_start(keep_dram[ds(k, 1), :, :].rearrange("b p n -> (b p) n"), keep[par][:, :]).then_inc(kept[par], 16)

            def step(f, par):
                if not is_int(f) or f < B - 1:
                    sp.wait_ge(x1_done, f)
                    sp.dma_start(xin[1 - par][:, :, :], x_v[ds(f + 1, 1), :, :].rearrange("b p (t n) -> (b p) t n", t=NT)).then_inc(x_loaded[1 - par], 16)
                store(f - 1, 1 - par)

            schedule(sp, step, store)

            sp.wait_ge(table_ready, 1)
            sp.wait_ge(pads_in, 16 * NE)
            sp.wait_ge(spare_in, 16)
            for i in range(2):
                sp.wait_ge(scattered[i], 16 * 2 * NT * (B // 2))

            def load_unit(n, i):
                row = sp.value_load(unit_row[0:1, ds(n, 1)], min_val=0, max_val=SLOTS - P)
                sp.dma_start(xb[i][:, :], slots_dram[ds(row, P), :]).then_inc(xb_in[i], 16)

            for i in range(QU):
                load_unit(i, i)
            with sp.Fori(1, UNITS // QU) as j:
                for i in range(QU):
                    sp.wait_ge(xbT_ps, of(j, QU, i - QU + 1))
                    sp.wait_ge(yi_sb, of(j, QU, i - QU + 1))
                    load_unit(j * QU + i, i)

            for i in range(2):
                sp.wait_ge(kept[i], 16 * (B // 2))
            for i in range(QU):
                sp.wait_ge(y_out[i], 16 * (UNITS // QU))

            def load_c(b, par):
                sp.dma_start(keep[par][:, :], keep_dram[ds(b, 1), :, :].rearrange("b p n -> (b p) n")).then_inc(c_in[par], 16)
                sp.dma_start(yin[par][:, :, :, :].rearrange("p t k n -> p (t k n)"), routed_v[ds(b, 1), :, :].rearrange("b p n -> (b p) n")).then_inc(c_in[par], 16)

            def store_c(b, par):
                sp.wait_ge(out_add, of(b, NT, NT))
                sp.dma_start(out_v[ds(b, 1), :, :].rearrange("b p n -> (b p) n"), res[par][:, :, :].rearrange("p t n -> p (t n)")).then_inc(stored[par], 16)

            load_c(0, 0)
            load_c(1, 1)
            with sp.Fori(0, (B - 2) // 2) as j:
                for i in range(2):
                    store_c(j * 2 + i, i)
                    load_c(j * 2 + i + 2, i)
            store_c(B - 2, 0)
            store_c(B - 1, 1)
            for i in range(2):
                sp.wait_ge(stored[i], 16 * (B // 2))

        @block.gpsimd
        def _(pool):
            g = nc.gpsimd
            n = [0]

            def link(ins):
                n[0] += 1
                ins.then_inc(setup, 1)

            link(g.memset(ident[:, :], 0.0))
            link(g.memset(ones[:, :], 1.0))
            link(g.memset(ones_bf[:, :], 1.0))
            link(g.memset(tri[:, :], 1.0))
            link(g.memset(head_mask[:, :], 1.0))
            link(g.memset(lower8[:, :, :], 1.0))
            link(g.memset(spare_rows[:, :, :], 0.0))
            link(g.memset(pad_rows[:, :, :], 0.0))
            link(g.memset(v1[:, :, E:E + 1], 1.0))
            link(g.memset(total[:, :], 0.0))
            link(g.memset(total_bf[:, :], 0.0))
            link(g.iota(rank_of[:, :], [[-1, NE]], base=NE, channel_multiplier=0, allow_small_or_imprecise_dtypes=True))
            for e in range(NE):
                link(g.memset(region[:, e:e + 1], float(e * CAP)))
            link(g.iota(tok2[:, :].rearrange("p (b t) -> p b t", b=B), [[2 * S, B], [2, NT]], base=0, channel_multiplier=2 * NT, allow_small_or_imprecise_dtypes=True))
            link(g.iota(unit_no[:, :], [[1, UNITS]], base=0, channel_multiplier=0, allow_small_or_imprecise_dtypes=True))
            link(g.iota(part_no[:, :], [[0, NE]], base=0, channel_multiplier=1, allow_small_or_imprecise_dtypes=True))
            pool.wait_ge(setup, n[0])
            link(g.affine_select(out=ident[:, :], in_=ident[:, :], compare_op=ALU.not_equal, fill=1.0, base=0, pattern=[[-1, P]], channel_multiplier=1))
            link(g.affine_select(out=tri[:, :], in_=tri[:, :], compare_op=ALU.is_gt, fill=0.0, base=0, pattern=[[1, P]], channel_multiplier=-1))
            link(g.affine_select(out=lower8[:, :, :], in_=lower8[:, :, :], compare_op=ALU.is_ge, fill=0.0, base=0, pattern=[[1, NE], [-1, NE]], channel_multiplier=0))
            link(g.affine_select(out=head_mask[:, :], in_=head_mask[:, :], compare_op=ALU.is_ge, fill=0.0, base=0, pattern=[[-D, HEADS]], channel_multiplier=1))
            link(g.iota(pad_rows[:, :, E:E + 1], [[2 * P, NE], [0, 1]], base=2 * TOK, channel_multiplier=2, allow_small_or_imprecise_dtypes=True))
            link(g.iota(spare_rows[:, :, E:E + 1], [[2, NE], [0, 1]], base=2 * TOK + 2 * NE * P, channel_multiplier=2 * NE, allow_small_or_imprecise_dtypes=True))
            pool.wait_ge(setup, n[0])
            g.affine_select(out=head_mask[:, :], in_=head_mask[:, :], compare_op=ALU.is_ge, fill=0.0, base=D - 1, pattern=[[D, HEADS]], channel_multiplier=-1).then_inc(consts, 1)

            def scatter(k, par):
                pool.wait_ge(slots_ready, of(k, 1, 1))
                pool.sem_inc(pool_passed, 1)
                for t in range(NT):
                    for c in range(2):
                        g.indirect_dma_start(slots_dram, bass.IndirectOffsetOnAxis(ap=slot_i[par][:, c * NT + t:c * NT + t + 1], axis=0),
                                             u_row[par][:, t, :], None).then_inc(scattered[par], 16)

            scatter(0, 0)
            with pool.Fori(0, (B - 2) // 2) as j:
                scatter(j * 2 + 1, 1)
                scatter(j * 2 + 2, 0)
            scatter(B - 1, 1)
            pool.wait_ge(pads_ready, 1)
            for e in range(NE):
                g.indirect_dma_start(slots_dram, bass.IndirectOffsetOnAxis(ap=pad_i[:, e:e + 1], axis=0), pad_rows[:, e, :], None).then_inc(pads_in, 16)

            def scatter_y(n_, i):
                pool.wait_ge(y_sb, n_ + TOK // P + 1)
                pool.wait_ge(yi_sb, n_ + 1)
                pool.sem_inc(pool_passed, 1)
                g.indirect_dma_start(routed_dram, bass.IndirectOffsetOnAxis(ap=yi[i][:, 0:1], axis=0), yb[i][:, :], None).then_inc(y_out[i], 16)

            with pool.Fori(0, UNITS // QU) as j:
                for i in range(QU):
                    scatter_y(j * QU + i, i)

        @block.tensor
        def _(pe):
            mm = nc.tensor.matmul
            pe.wait_ge(consts, 1)
            pe.wait_ge(setup_ps, 1)
            mm(bank_h[0][:, 0:NE], ones[:, :], gate_s[:, :], start=True, stop=True)
            mm(bank_h[0][:, NE:2 * NE], ln_bi_w[:, :], gate_t[:, :], start=True, stop=True).then_inc(setup_ps, 1)

            def attn(k):
                pe.wait_ge(kvm_sb, of(k, 1, 1))
                pe.wait_ge(pq_sb, of(k, 2, 2))
                for i in range(4):
                    if i < 2:
                        pe.wait_ge(pk_sb, of(k, 4, 4))
                    else:
                        pe.wait_ge(att_sb, of(k, 4, i - 1))
                    for h in range(2):
                        t = 2 * i + h
                        last = mm(bank_p[i % 2][:, 256 * h:256 * h + E + HEADS], pqT[:, t * P:(t + 1) * P], kvm[:, :], start=True, stop=True)
                    last.then_inc(attn_ps, 1)

            def front(f):
                pe.wait_ge(xn_sb, of(f, 1, 1))
                for i in range(2):
                    if is_int(f) and f < 2:
                        if f == 1:
                            pe.wait_ge(kvm_sb, 1)
                            pe.wait_ge(xnT_sb, 2)
                    elif i == 0:
                        pe.wait_ge(uT_sb, of(f, 2, -3))
                    else:
                        pe.wait_ge(slots_ready, of(f, 1, -1))
                    for t in range(4 * i, 4 * i + 4):
                        last = nc.tensor.transpose(bank_t[i][:, (t % 4) * P:(t % 4 + 1) * P], xn[:, t, :], ident[:, :])
                    last.then_inc(xnT_ps, 1)
                for i in range(2):
                    pe.wait_ge(xnT_sb, of(f, 2, i + 1))
                    if not is_int(f) or f > 0:
                        pe.wait_ge(att_sb, of(f, 4, i - 1))
                    mm(bank_p[i][:, :], bias_bf[:, 0:E], ones_bf[:, :], start=True, stop=False)
                    mm(bank_p[i][:, :], wqkv[:, 0:E], xnT[:, i * 512:(i + 1) * 512], start=False, stop=True).then_inc(q_ps, 1)
                for i in range(4):
                    if i < 2:
                        pe.wait_ge(pq_sb, of(f, 2, i + 1))
                    else:
                        pe.wait_ge(pk_sb, of(f, 4, i - 1))
                    for h in range(2):
                        t = 2 * i + h
                        o = bank_p[i % 2][:, 256 * h:256 * h + 256]
                        mm(o, ones_bf[:, 0:P], bias_bf[:, E:3 * E], start=True, stop=False)
                        last = mm(o, xnT[:, t * P:(t + 1) * P], wqkv[:, E:3 * E], start=False, stop=True)
                    last.then_inc(kv_ps, 1)
                for t in range(NT):
                    if t % 2 == 0:
                        pe.wait_ge(pk_sb, of(f, 4, t // 2 + 1))
                    last = mm(bank_t[0][:, 0:E + 1], pk[:, t, :], v1[:, t, :], start=t == 0, stop=t == NT - 1)
                last.then_inc(sum_ps, 1)

            def gate_up(n_, i, xT, w):
                if not is_int(n_) or n_ >= 2:
                    pe.wait_ge(hid_sb, n_ - 1)
                mm(bank_g[i][:, :], xT, w, start=True, stop=True).then_inc(gu_ps, 1)

            def hid_t(n_, i):
                pe.wait_ge(hid_sb, n_ + 1)
                if not is_int(n_) or n_ >= 2:
                    pe.wait_ge(ht_sb, n_ - 1)
                for c in range(IC):
                    last = nc.tensor.transpose(bank_h[i][:, c * P:(c + 1) * P], hid[:, i, c * P:(c + 1) * P], ident[:, :])
                last.then_inc(ht_ps, 1)

            def down(n_, i, w):
                pe.wait_ge(ht_sb, n_ + 1)
                if not is_int(n_) or n_ >= 2:
                    pe.wait_ge(y_sb, n_ - 1)
                for c in range(IC):
                    last = mm(bank_h[i][:, INTER:INTER + E], hidT[:, i, c * P:(c + 1) * P], w(c), start=c == 0, stop=c == IC - 1)
                last.then_inc(y_ps, 1)

            def back(k, par):
                for i in range(2):
                    pe.wait_ge(u_sb, of(k, 2, i + 1))
                    if not is_int(k) or k < B - 1:
                        if i == 0:
                            pe.wait_ge(kvm_sb, of(k, 1, 2))
                        else:
                            pe.wait_ge(xnT_sb, of(k, 2, 4))
                    else:
                        if i == 1:
                            pe.wait_ge(slots_ready, k)
                    for t in range(4 * i, 4 * i + 4):
                        last = nc.tensor.transpose(bank_t[i][:, (t % 4) * P:(t % 4 + 1) * P], u_row[par][:, t, 0:E], ident[:, :])
                    last.then_inc(uT_ps, 1)
                pe.wait_ge(uT_sb, of(k, 2, 2))
                for t in range(NT):
                    last = mm(bank_t[1][:, t * NE:(t + 1) * NE], uT[:, t * P:(t + 1) * P], gate_c[:, :], start=True, stop=True)
                last.then_inc(logit_ps, 1)
                for t in range(NT + 2):
                    n_ = k * NT + t
                    if t < NT:
                        gate_up(n_, t % 2, uT[:, t * P:(t + 1) * P], swgu[:, :])
                    if t >= 2:
                        down(n_ - 2, t % 2, lambda c: swdn[:, c * E:(c + 1) * E])
                    if 1 <= t <= NT:
                        hid_t(n_ - 1, (t - 1) % 2)
                    if t == 4:
                        pe.wait_ge(oh_ready, of(k, 1, 1))
                        o = bank_t[1]
                        oh = oh_bf[:, :, :].rearrange("p t e -> p (t e)")
                        mm(o[:, 64:128], tri[:, :], oh, start=True, stop=False)
                        for s in range(1, NT):
                            mm(o[:, 64 + s * NE:128], ones_bf[:, 0:P], oh[:, 0:(NT - s) * NE], start=False, stop=False)
                        mm(o[:, 64:128], ones_bf[:, 0:P], total_bf[:, :].unsqueeze(1).to_broadcast([P, NT, NE]), start=False, stop=True).then_inc(rank_ps, 1)

            def step(f, par):
                attn(f - 1)
                front(f)
                back(f - 1, 1 - par)

            def last_back(k, par):
                attn(k)
                back(k, par)

            pe.wait_ge(setup_ps, 3)
            pe.wait_ge(w_loaded, 16 * 7)
            front(0)
            pe.wait_ge(sw_loaded, 16 * 3)
            schedule(pe, step, last_back)

            pe.wait_ge(oh_ready, B + 1)
            mm(bank_t[0][:, 0:NE], ones_bf[:, 0:P], total_bf[:, :], start=True, stop=True).then_inc(cnt_ps, 1)

            N0 = TOK // P
            pe.wait_ge(ew_loaded, 16 * (2 + NE))
            pe.wait_ge(table_ready, 1)

            def unit(j, i, first, final):
                n_ = j * QU + i
                e = pe.value_load(unit_e[0:1, ds(n_, 1)], min_val=0, max_val=NE - 1)
                pe.wait_ge(xbT_sb, n_ + 1)
                pe.wait_ge(hid_sb, n_ + N0 - 1)
                mm(bank_g[i % 2][:, :], xbT[:, i % 2, :], wgu[:, ds(e, 1), :].rearrange("p e n -> p (e n)"), start=True, stop=True).then_inc(gu_ps, 1)
                if not (final and i == QU - 1):
                    nx = (i + 1) % QU
                    pe.wait_ge(xb_in[nx], (j + (i + 1) // QU) * 16 + 16)
                    if not first or i >= 1:
                        pe.wait_ge(xbT_sb, n_)
                    nc.tensor.transpose(bank_t[nx % 2][:, 0:E], xb[nx][:, 0:E], ident[:, :]).then_inc(xbT_ps, 1)
                if not first or i >= 2:
                    routed_down(n_ - 2, i % 2)
                if not first or i >= 1:
                    hid_t(n_ + N0 - 1, (i + 1) % 2)

            def routed_down(n_, i):
                e = pe.value_load(unit_e[0:1, ds(n_, 1)], min_val=0, max_val=NE - 1)
                down(n_ + N0, i, lambda c: wdn[:, ds(e, 1), c * E:(c + 1) * E].rearrange("p e n -> p (e n)"))

            pe.wait_ge(xb_in[0], 16)
            nc.tensor.transpose(bank_t[0][:, 0:E], xb[0][:, 0:E], ident[:, :]).then_inc(xbT_ps, 1)
            NJ = UNITS // QU
            for i in range(QU):
                unit(0, i, True, False)
            with pe.Fori(1, NJ - 1) as j:
                for i in range(QU):
                    unit(j, i, False, False)
            for i in range(QU):
                unit(NJ - 1, i, False, True)
            routed_down(UNITS - 2, UNITS % 2)
            hid_t(UNITS - 1 + N0, (UNITS - 1) % 2)
            routed_down(UNITS - 1, (UNITS - 1) % 2)

        @block.scalar
        def _(act):
            A = nc.scalar.activation

            def front(f):
                for i in range(2):
                    act.wait_ge(xnT_ps, of(f, 2, i + 1))
                    A(xnT[:, i * 512:(i + 1) * 512], bank_t[i][:, :], ACT.Copy).then_inc(xnT_sb, 1)
                for i in range(2):
                    act.wait_ge(q_ps, of(f, 2, i + 1))
                    A(q_e[:, i, :], bank_p[i][:, :], ACT.Exp, bias=minus1[:, 0:1]).then_inc(q_exp, 1)
                for i in range(4):
                    act.wait_ge(kv_ps, of(f, 4, i + 1))
                    o = bank_p[i % 2][:, :].rearrange("p (h n) -> p h n", h=2)
                    A(v1[:, 2 * i:2 * i + 2, 0:E], o[:, :, E:2 * E], ACT.Copy)
                    A(k_e[:, i % 2, :, :], o[:, :, 0:E], ACT.Exp, bias=minus1[:, 0:1]).then_inc(kv_exp, 1)

            def silu_of(n_, i):
                act.wait_ge(gu_ps, n_ + 1)
                A(act_g[:, i, :], bank_g[i][:, 0:INTER], ACT.Silu).then_inc(silu, 1)

            def ht_of(n_, i):
                act.wait_ge(ht_ps, n_ + 1)
                A(hidT[:, i, :], bank_h[i][:, 0:INTER], ACT.Copy).then_inc(ht_sb, 1)

            def back(k, par):
                for i in range(2):
                    act.wait_ge(uT_ps, of(k, 2, i + 1))
                    A(uT[:, i * 512:(i + 1) * 512], bank_t[i][:, :], ACT.Copy).then_inc(uT_sb, 1)
                for t in range(NT + 2):
                    n_ = k * NT + t
                    if t < NT:
                        silu_of(n_, t % 2)
                    if t >= 2:
                        act.wait_ge(y_ps, n_ - 1)
                        A(keep[par][:, (NT + t - 2) * E:(NT + t - 1) * E], bank_h[t % 2][:, INTER:INTER + E], ACT.Copy).then_inc(y_sb, 1)
                    if 1 <= t <= NT:
                        ht_of(n_ - 1, (t - 1) % 2)
                act.wait_ge(r_ready, of(k, 1, 1))
                A(r_exp[:, :, :], r_in[:, :, :], ACT.Exp).then_inc(r_done, 1)

            def step(f, par):
                front(f)
                back(f - 1, 1 - par)

            act.wait_ge(setup_ps, 3)
            front(0)
            schedule(act, step, back)

            N0 = TOK // P

            def unit(j, i, first):
                n_ = j * QU + i
                silu_of(n_ + N0, i % 2)
                if not first or i >= 2:
                    y_of(n_ - 2, (i - 2) % QU, j, first)
                if not first or i >= 1:
                    ht_of(n_ + N0 - 1, (i - 1) % 2)

            def y_of(n_, i, j, first):
                act.wait_ge(y_ps, n_ + N0 + 1)
                if not first:
                    act.wait_ge(y_out[i], (j - (1 if i >= 2 else 0)) * 16)
                A(yb[i][:, :], bank_h[i % 2][:, INTER:INTER + E], ACT.Copy).then_inc(y_sb, 1)

            for i in range(QU):
                unit(0, i, True)
            for i in range(QU):
                n_ = QU + i
                silu_of(n_ + N0, i % 2)
                y_of(n_ - 2, (i - 2) % QU, 1, i < 2)
                ht_of(n_ + N0 - 1, (i - 1) % 2)
            with act.Fori(2, UNITS // QU) as j:
                for i in range(QU):
                    unit(j, i, False)
            y_of(UNITS - 2, (UNITS - 2) % QU, UNITS // QU, False)
            ht_of(UNITS - 1 + N0, (UNITS - 1) % 2)
            y_of(UNITS - 1, (UNITS - 1) % QU, UNITS // QU, False)

            def final(b, par):
                for t in range(NT):
                    act.wait_ge(res_ready, of(b, NT, t + 1))
                    A(res[par][:, t, :], res[par][:, t, :], ACT.Identity, bias=shift[:, t:t + 1]).then_inc(out_add, 1)

            with act.Fori(0, B // 2) as j:
                final(j * 2, 0)
                final(j * 2 + 1, 1)

        @block.vector
        def _(dv):
            v = nc.vector
            base, n = [0], [0]

            def inc(ins):
                n[0] += 1
                ins.then_inc(dve, 1)
                return n[0]

            def wait(k=None):
                dv.wait_ge(dve, base[0] + (n[0] if k is None else k))

            def link(ins):
                inc(ins)
                wait()

            def rsqrt(dst, var, w, filler=()):
                it = iter(filler)

                def go(ins):
                    k = inc(ins)
                    for fn in it:
                        fn()
                        break
                    wait(k)

                go(v.tensor_scalar(dst.bitcast(i32), var.bitcast(i32), -0.5, float(0x5f3759df), ALU.mult, ALU.add))
                t = nt_[:, 0:w]
                for _ in range(3):
                    go(v.tensor_tensor(t, dst, dst, ALU.mult))
                    go(v.scalar_tensor_tensor(out=t, in0=t, scalar=-0.5, in1=var, op0=ALU.mult, op1=ALU.mult))
                    go(v.scalar_tensor_tensor(out=dst, in0=t, scalar=1.5, in1=dst, op0=ALU.add, op1=ALU.mult))
                for fn in it:
                    fn()

            def stats(src, st):
                for t in range(NT):
                    last = v.bn_stats(st[:, t, :], src(t))
                link(last)

            def aggr(st, mv):
                dv.sem_inc(dve_passed, 1)
                for t in range(NT):
                    last = v.bn_aggr(mv[:, t, :], st[:, t, :])
                link(last)

            minus_one = v.memset(minus1[:, :], -1.0)
            inc(minus_one)
            link(v.memset(bias_acc[:, :], 0.0))
            link(v.memset(bias_bf[:, :], 0.0))
            dv.wait_ge(consts, 1)
            dv.wait_ge(w_loaded, 16 * 7)
            link(v.tensor_scalar(bias3[0:3, 0:2 * E], bias3[0:3, 0:2 * E], 1.0, None, ALU.add))
            for i in range(3):
                link(v.tensor_copy(bias_part[0:3, :], bias3[0:3, :]))
                link(v.scalar_tensor_tensor(out=bias_acc[0:3, :], in0=bias_part[0:3, :], scalar=ident[0:3, i:i + 1], in1=bias_acc[0:3, :], op0=ALU.mult, op1=ALU.add))
                if i < 2:
                    link(v.tensor_tensor(bias3[0:3, :], bias3[0:3, :], bias_part[0:3, :], ALU.subtract))
            link(v.tensor_copy(bias_bf[0:3, :], bias_acc[0:3, :]))
            v.tensor_scalar(gate_s[:, :], gate_t[:, :], ln_sc[:, 0:1], None, ALU.mult)
            v.tensor_scalar(ln_bi_w[:, :], ones[:, :], ln_bi[:, 0:1], None, ALU.mult).then_inc(setup_ps, 1)
            dv.wait_ge(setup_ps, 2)
            v.tensor_copy(gate_b[:, :], bank_h[0][:, NE:2 * NE])
            v.scalar_tensor_tensor(out=gate_c[:, :], in0=bank_h[0][:, 0:NE], scalar=-1.0 / E, in1=gate_s[:, :], op0=ALU.mult, op1=ALU.add).then_inc(setup_ps, 1)

            def ln1(f, par, combined):
                xt = xin[par]
                dv.wait_ge(x_loaded[par], (f - par) * 8 + 16)
                stats(lambda t: xt[:, t, :], st_1)
                aggr(st_1, mv_1)
                link(v.tensor_scalar(ve[:, NT:2 * NT], mv_1[:, :, 1], LN_EPS, None, ALU.add))
                if not combined:
                    rsqrt(r_41[:, NT:2 * NT], ve[:, NT:2 * NT], NT)

            def xn_of(t, par, last=False):
                ins = v.tensor_scalar(xn[:, t, :], xin[par][:, t, :], mv_1[:, t, 0:1], r_41[:, NT + t:NT + t + 1], ALU.subtract, ALU.mult)
                if last:
                    ins.then_inc(xn_sb, 1)

            def phi_q(f, i):
                dv.wait_ge(q_exp, of(f, 2, i + 1))
                v.scalar_tensor_tensor(out=pqT[:, i * 512:(i + 1) * 512], in0=q_e[:, i, :], scalar=1.0, in1=bank_p[i][:, :],
                                       op0=ALU.min, op1=ALU.max).then_inc(pq_sb, 1)

            def phi_k(f, i):
                dv.wait_ge(kv_exp, of(f, 4, i + 1))
                v.scalar_tensor_tensor(out=pk[:, 2 * i:2 * i + 2, :], in0=k_e[:, i % 2, :, :], scalar=1.0,
                                       in1=bank_p[i % 2][:, :].rearrange("p (h n) -> p h n", h=2)[:, :, 0:E],
                                       op0=ALU.min, op1=ALU.max).then_inc(pk_sb, 1)

            def kv_mask(f):
                dv.wait_ge(sum_ps, of(f, 1, 1))
                v.tensor_tensor(kvm[:, 0:E].rearrange("p (h m) -> p h m", m=D), bank_t[0][:, 0:E].rearrange("p (h m) -> p h m", m=D),
                                head_mask[:, :].unsqueeze(2).to_broadcast([P, HEADS, D]), ALU.mult)
                v.tensor_scalar(kvm[:, E:E + HEADS], head_mask[:, :], bank_t[0][:, E:E + 1], None, ALU.mult).then_inc(kvm_sb, 1)

            def back(k, par, f):
                kp = keep[par]
                x1 = kp[:, 0:NT * E].rearrange("p (t n) -> p t n", n=E)
                fill = []
                if f is not None:
                    fill = [lambda i=i: phi_q(f, i) for i in range(2)] + [lambda i=i: phi_k(f, i) for i in range(4)] + [lambda: kv_mask(f)]
                for i in range(4):
                    dv.wait_ge(attn_ps, of(k, 4, i + 1))
                    a = bank_p[i % 2][:, :].rearrange("p (h n) -> p h n", h=2)
                    link(v.tensor_scalar(zt[:, i % 2, :, :], a[:, :, E:E + HEADS], 1e-6, None, ALU.add))
                    link(v.reciprocal(zr[:, i % 2, :, :], zt[:, i % 2, :, :]))
                    for h in range(2):
                        last = v.tensor_tensor(att[:, 2 * i + h, :].rearrange("p (h m) -> p h m", m=D), a[:, h, 0:E].rearrange("p (h m) -> p h m", m=D),
                                               zr[:, i % 2, h, :].unsqueeze(2).to_broadcast([P, HEADS, D]), ALU.mult)
                    last.then_inc(att_sb, 1)
                dv.wait_ge(att_sb, of(k, 4, 4))
                stats(lambda t: att[:, t, :], st_a)
                aggr(st_a, mv_a)
                link(v.tensor_scalar(ve[:, 0:NT], mv_a[:, :, 1], LN_EPS, None, ALU.add))
                rsqrt(r_a[:, :], ve[:, 0:NT], NT, fill[0:2])
                if not is_int(k) or k >= 2:
                    dv.wait_ge(kept[par], kept_at(k, par))
                for t in range(NT):
                    last = v.scalar_tensor_tensor(out=x1[:, t, :], in0=att[:, t, :], scalar=r_a[:, t:t + 1], in1=xin[par][:, t, :], op0=ALU.mult, op1=ALU.add)
                    if fill and t in (3, 5):
                        fill[2 + t // 5]()
                last.then_inc(x1_done, 1)
                v.scalar_tensor_tensor(out=kp[:, 2 * NT * E:2 * NT * E + NT], in0=mv_a[:, :, 0], scalar=-1.0, in1=r_a[:, :], op0=ALU.mult, op1=ALU.mult)
                dv.wait_ge(x1_done, of(k, 1, 1))
                stats(lambda t: x1[:, t, :], st_a)
                aggr(st_a, mv_u)
                link(v.tensor_scalar(ve[:, 0:NT], mv_u[:, :, 1], LN_EPS, None, ALU.add))
                rsqrt(r_u[:, :], ve[:, 0:NT], NT, fill[4:7])
                if not is_int(k) or k >= 2:
                    dv.wait_ge(scattered[par], scattered_at(k, par))
                for t in range(NT):
                    last = v.tensor_scalar(u_row[par][:, t, 0:E], x1[:, t, :], mv_u[:, t, 0:1], r_u[:, t:t + 1], ALU.subtract, ALU.mult)
                    if t % 4 == 3:
                        last.then_inc(u_sb, 1)
                link(v.tensor_tensor(ve[:, 0:NT], mv_u[:, :, 1], r_u[:, :], ALU.mult))
                link(v.tensor_tensor(ve[:, 0:NT], ve[:, 0:NT], r_u[:, :], ALU.mult))
                inc(v.tensor_scalar(ve[:, 0:NT], ve[:, 0:NT], LN_EPS, None, ALU.add))
                more = f is not None and (not is_int(f) or f < B - 1)
                if more:
                    ln1(f + 1, par, True)
                    wait()
                    rsqrt(r_41[:, :], ve[:, :], 2 * NT)
                    for t in range(NT):
                        xn_of(t, par, t == NT - 1)
                else:
                    wait()
                    rsqrt(r_41[:, 0:NT], ve[:, 0:NT], NT)
                units = iter([lambda t=t: hidden(k * NT + t, t % 2) for t in range(NT)])

                def bc(a):
                    return a.unsqueeze(2).to_broadcast([P, NT, NE])

                def per_e(a):
                    return a.unsqueeze(1).to_broadcast([P, NT, NE])

                def lk(ins):
                    k_ = inc(ins)
                    count[0] += 1
                    if count[0] % 3 == 0:
                        for fn in units:
                            fn()
                            break
                    wait(k_)

                count = [0]
                dv.wait_ge(logit_ps, of(k, 1, 1))
                lk(v.tensor_tensor(lg[:, :, :], bank_t[1][:, 0:NT * NE].rearrange("p (t e) -> p t e", e=NE), bc(r_41[:, 0:NT]), ALU.mult))
                lk(v.tensor_tensor(lg[:, :, :], lg[:, :, :], per_e(gate_b[:, :]), ALU.add))
                lk(v.tensor_reduce(m1[:, :], lg[:, :, :], AX.X, ALU.max))
                lk(v.tensor_tensor(cand[:, :, :], lg[:, :, :], bc(m1[:, :]), ALU.is_equal))
                lk(v.tensor_tensor(cand[:, :, :], cand[:, :, :], per_e(rank_of[:, :]), ALU.mult))
                lk(v.tensor_reduce(i1[:, :], cand[:, :, :], AX.X, ALU.max))
                lk(v.tensor_tensor(oh1[:, :, :], per_e(rank_of[:, :]), bc(i1[:, :]), ALU.is_equal))
                lk(v.scalar_tensor_tensor(out=lg2[:, :, :], in0=oh1[:, :, :], scalar=-3e38, in1=lg[:, :, :], op0=ALU.mult, op1=ALU.add))
                lk(v.tensor_reduce(m2[:, :], lg2[:, :, :], AX.X, ALU.max))
                v.tensor_tensor(r_in[:, :, 0:NE], lg[:, :, :], bc(m1[:, :]), ALU.subtract)
                v.tensor_tensor(r_in[:, :, NE], m2[:, :], m1[:, :], ALU.subtract).then_inc(r_ready, 1)
                lk(v.tensor_tensor(cand[:, :, :], lg2[:, :, :], bc(m2[:, :]), ALU.is_equal))
                lk(v.tensor_tensor(cand[:, :, :], cand[:, :, :], per_e(rank_of[:, :]), ALU.mult))
                lk(v.tensor_reduce(i2[:, :], cand[:, :, :], AX.X, ALU.max))
                lk(v.tensor_tensor(oh2[:, :, :], per_e(rank_of[:, :]), bc(i2[:, :]), ALU.is_equal))
                v.tensor_tensor(oh_bf[:, :, :], oh1[:, :, :], oh2[:, :, :], ALU.add).then_inc(oh_ready, 1)
                v.tensor_scalar(u_row[par][:, :, E + 1], i1[:, :], -1.0, float(NE), ALU.mult, ALU.add)
                tail = v.tensor_copy(u_row[par][:, :, E], tok2[:, ds(k * NT, NT)])
                inc(tail)
                return list(units)

            def kept_at(k, par):
                return (k - par) * 8

            def scattered_at(k, par):
                return (k - par) * (8 * 2 * NT)

            def hidden(n_, i):
                dv.wait_ge(silu, n_ + 1)
                v.tensor_tensor(hid[:, i, :], act_g[:, i, :], bank_g[i][:, INTER:2 * INTER], ALU.mult).then_inc(hid_sb, 1)

            def back_end(k, par, rest):
                kp = keep[par]
                done = NT - len(rest)
                while done < 5:
                    rest.pop(0)()
                    done += 1
                dv.wait_ge(oh_ready, of(k, 1, 1))
                link(v.tensor_reduce(total_new[:, :], oh_bf[:, :, :].rearrange("p t e -> p e t"), AX.X, ALU.add))
                dv.wait_ge(rank_ps, of(k, 1, 1))
                inc(v.tensor_tensor(total[:, :], total[:, :], total_new[:, :], ALU.add))
                link(v.tensor_tensor(pos[:, :, :], bank_t[1][:, 64:128].rearrange("p (t e) -> p t e", e=NE), region[:, :].unsqueeze(1).to_broadcast([P, NT, NE]), ALU.add))
                inc(v.tensor_copy(total_bf[:, :], total[:, :]))
                inc(v.tensor_tensor(oh1[:, :, :], oh1[:, :, :], pos[:, :, :], ALU.mult))
                link(v.tensor_tensor(oh2[:, :, :], oh2[:, :, :], pos[:, :, :], ALU.mult))
                inc(v.tensor_reduce(slot_f[:, 0:NT], oh1[:, :, :], AX.X, ALU.add))
                link(v.tensor_reduce(slot_f[:, NT:2 * NT], oh2[:, :, :], AX.X, ALU.add))
                v.tensor_copy(slot_i[par][:, :], slot_f[:, :]).then_inc(slots_ready, 1)
                for fn in rest:
                    fn()
                dv.wait_ge(r_done, of(k, 1, 1))
                link(v.tensor_reduce(esum[:, :], r_exp[:, :, 0:NE], AX.X, ALU.add))
                link(v.scalar_tensor_tensor(out=den[:, :], in0=esum[:, :], scalar=EPS, in1=r_exp[:, :, NE], op0=ALU.mult, op1=ALU.add))
                link(v.tensor_scalar(den[:, :], den[:, :], 1.0, None, ALU.add))
                w0 = 2 * NT * E + NT
                link(v.reciprocal(kp[:, w0:w0 + NT], den[:, :]))
                v.tensor_tensor(kp[:, w0 + NT:w0 + 2 * NT], kp[:, w0:w0 + NT], r_exp[:, :, NE], ALU.mult).then_inc(keep_ready, 1)

            def step(f, par):
                back_end(f - 1, 1 - par, back(f - 1, 1 - par, f))

            ln1(0, 0, False)
            for t in range(NT):
                xn_of(t, 0, t == NT - 1)
            phi_q(0, 0)
            phi_q(0, 1)
            for i in range(4):
                phi_k(0, i)
            kv_mask(0)
            dv.wait_ge(xnT_ps, 2)
            ln1(1, 1, False)
            for t in range(NT):
                xn_of(t, 1, t == NT - 1)
            step(1, 1)
            step(2, 0)
            start = base[0] + n[0]
            LOOPS = (B - 4) // 2
            with dv.Fori(0, LOOPS) as j:
                base[0], n[0] = j * DVE_PAIR + start, 0
                step(j * 2 + 3, 1)
                step(j * 2 + 4, 0)
                assert n[0] == DVE_PAIR, f"DVE_PAIR = {n[0]}"
            base[0], n[0] = start + LOOPS * DVE_PAIR, 0
            step(B - 1, 1)
            back_end(B - 1, 1, back(B - 1, 1, None))
            dv.wait_ge(slots_ready, B)
            v.tensor_copy(total_bf[:, :], total[:, :]).then_inc(oh_ready, 1)

            dv.wait_ge(cnt_ps, 1)
            link(v.tensor_copy(cnt[:, :], bank_t[0][:, 0:NE]))
            inc(v.tensor_tensor(pad_f[:, :], cnt[:, :], region[:, :], ALU.add))
            link(v.tensor_scalar(tl_i[:, :], cnt[:, :], float(P - 1), None, ALU.add))
            inc(v.tensor_tensor(pad_f[:, :], pad_f[:, :], part_no[:, :], ALU.add))
            link(v.tensor_scalar(tl_s[:, :], tl_i[:, :], 7, None, ALU.arith_shift_right))
            v.tensor_copy(pad_i[:, :], pad_f[:, :]).then_inc(pads_ready, 1)
            link(v.tensor_copy(tl[:, :], tl_s[:, :]))
            inc(v.tensor_scalar(gain[:, :], tl[:, :], float(-P), float(CAP + (1 << SHIFT)), ALU.mult, ALU.add))
            link(v.tensor_tensor(tl8[:, :, :], lower8[:, :, :], tl[:, :].unsqueeze(1).to_broadcast([P, NE, NE]), ALU.mult))
            link(v.tensor_reduce(cum[:, :], tl8[:, :, :], AX.X, ALU.add))
            link(v.tensor_tensor(past[:, :, :], unit_no[:, :].unsqueeze(2).to_broadcast([P, UNITS, NE]),
                                 cum[:, :].unsqueeze(1).to_broadcast([P, UNITS, NE]), ALU.is_ge))
            link(v.tensor_tensor(past[:, :, :], past[:, :, :], gain[:, :].unsqueeze(1).to_broadcast([P, UNITS, NE]), ALU.mult))
            link(v.tensor_reduce(pk_sum[:, :], past[:, :, :], AX.X, ALU.add))
            link(v.scalar_tensor_tensor(out=pk_i[:, :], in0=unit_no[:, :], scalar=float(P), in1=pk_sum[:, :], op0=ALU.mult, op1=ALU.add))
            inc(v.tensor_scalar(unit_row[:, :], pk_i[:, :], (1 << SHIFT) - 1, None, ALU.bitwise_and))
            link(v.tensor_scalar(unit_w[:, :], pk_i[:, :], SHIFT, None, ALU.arith_shift_right))
            inc(v.tensor_copy(unit_ef[:, :], unit_w[:, :]))
            v.tensor_scalar(unit_e[:, :], unit_w[:, :], float(NE - 1), None, ALU.min).then_inc(table_ready, 1)
            wait()

            N0 = TOK // P

            def x_copy(j, i, first):
                n_ = j * QU + i
                dv.wait_ge(xbT_ps, n_ + 1)
                v.tensor_copy(xbT[:, i % 2, :], bank_t[i % 2][:, 0:E]).then_inc(xbT_sb, 1)
                if not first:
                    dv.wait_ge(y_out[i], j * 16)
                v.tensor_scalar(yi[i][:, :], xb[i][:, E + 1:E + 2], unit_ef[:, ds(n_, 1)], xb[i][:, E:E + 1], ALU.not_equal, ALU.add).then_inc(yi_sb, 1)

            dv.wait_ge(xb_in[0], 16)
            x_copy(0, 0, True)
            for i in range(1, QU):
                x_copy(0, i, True)
                hidden(N0 + i - 1, (i - 1) % 2)
            with dv.Fori(1, UNITS // QU) as j:
                for i in range(QU):
                    x_copy(j, i, False)
                    hidden(j * QU + (i + N0 - 1), (i - 1) % 2)
            hidden(UNITS - 1 + N0, (UNITS - 1) % 2)

            def combine(b, par):
                kp = keep[par]
                w0 = 2 * NT * E + NT
                y = yin[par]
                dv.wait_ge(c_in[par], (b - par) * 16 + 32)
                for t in range(NT):
                    last = v.scalar_tensor_tensor(out=y[:, t, 0, :], in0=y[:, t, 0, :], scalar=kp[:, w0 + t:w0 + t + 1], in1=kp[:, (NT + t) * E:(NT + t + 1) * E], op0=ALU.mult, op1=ALU.add)
                link(last)
                for t in range(NT):
                    last = v.scalar_tensor_tensor(out=y[:, t, 0, :], in0=y[:, t, 1, :], scalar=kp[:, w0 + NT + t:w0 + NT + t + 1], in1=y[:, t, 0, :], op0=ALU.mult, op1=ALU.add)
                link(last)
                stats(lambda t: y[:, t, 0, :], st_a)
                aggr(st_a, mv_a)
                link(v.tensor_scalar(ve[:, 0:NT], mv_a[:, :, 1], LN_EPS, None, ALU.add))
                rsqrt(r_a[:, :], ve[:, 0:NT], NT)
                link(v.tensor_tensor(ve[:, 0:NT], mv_a[:, :, 0], r_a[:, :], ALU.mult))
                if not is_int(b) or b >= 1:
                    dv.wait_ge(out_add, of(b, NT))
                v.tensor_tensor(shift[:, :], kp[:, 2 * NT * E:2 * NT * E + NT], ve[:, 0:NT], ALU.subtract)
                if not is_int(b) or b >= 2:
                    dv.wait_ge(stored[par], (b - par) * 8)
                for t in range(NT):
                    v.scalar_tensor_tensor(out=res[par][:, t, :], in0=y[:, t, 0, :], scalar=r_a[:, t:t + 1], in1=kp[:, t * E:(t + 1) * E], op0=ALU.mult, op1=ALU.add).then_inc(res_ready, 1)

            combine(0, 0)
            combine(1, 1)
            start = base[0] + n[0]
            with dv.Fori(1, B // 2) as j:
                base[0], n[0] = (j - 1) * DVE_C + start, 0
                combine(j * 2, 0)
                combine(j * 2 + 1, 1)
                assert n[0] == DVE_C, f"DVE_C = {n[0]}"


_INS = ['L0_attn_x', 'L0_attn_W_qkv', 'L0_attn_b_qkv', 'L0_attn_W_proj', 'L0_attn_b_proj', 'L0_ffn_ln_scale',
        'L0_ffn_ln_bias', 'L0_ffn_gate_w', 'L0_ffn_Wg', 'L0_ffn_Wu', 'L0_ffn_Wd', 'L0_ffn_sWg', 'L0_ffn_sWu', 'L0_ffn_sWd']


def kernel(**inputs):
    import numpy as _np
    import concourse.bacc as _bacc
    from concourse import mybir as _mybir
    from concourse.bass_utils import run_bass_kernel_spmd as _run

    nc = _bacc.Bacc("TRN2", target_bir_lowering=False, num_devices=1)
    arrays, args = {}, []
    for name in _INS:
        a = _np.ascontiguousarray(inputs[name])
        arrays[f"in_{name}"] = a
        args.append(nc.dram_tensor(f"in_{name}", a.shape, _mybir.dt.from_np(a.dtype), kind="ExternalInput").ap())
    args.append(nc.dram_tensor("out_dram", (B, S, E), _mybir.dt.float32, kind="ExternalOutput").ap())
    program(nc, *args)
    r = _run(nc, [arrays], core_ids=[0])
    return r.results[0]["out_dram"]
```

```python
import concourse.bass as bass
from concourse import mybir
from contextlib import ExitStack

P = 128
E = 128
B, S = 8, 1024
NT = S // P
HEADS, D = 16, 8
INTER = 256
IC = INTER // P
NE = 8
TOK = B * S
CAP = TOK + P
ROW = E + 4
UNITS = 2 * TOK // P + NE
SLOTS = NE * CAP + NE * P
PADS = 2 * (NE * P + NE * P)
QU = 8
LN_EPS = 1e-5
EPS = 1e-5
SHIFT = 17
PHI_AT = (22, 26, 30, 33, 36, 39, 44)
ROUTER_AT = tuple(range(8, 26))
PRODUCTS_AT = tuple(range(50, 106, 7))
DISPATCH_AT = tuple(range(66, 100, 4))
DVE_PAIR = 230
DVE_C = 88
KEEP = 2 * NT * E + NT


def program(nc, x, w_qkv, b_qkv, w_proj, b_proj, ln_scale, ln_bias, gate_w, wg, wu, wd, swg, swu, swd, out):
    f32, bf16, i32 = mybir.dt.float32, mybir.dt.bfloat16, mybir.dt.int32
    ALU, ACT, AX = mybir.AluOpType, mybir.ActivationFunctionType, mybir.AxisListType
    ds = bass.ds

    x_v = x.rearrange("b (p t) f -> b p (t f)", t=NT)
    out_v = out.rearrange("b (p t) f -> b p (t f)", t=NT)
    slots_dram = nc.dram_tensor("slots_dram", (SLOTS, ROW), f32, kind="Internal").ap()
    routed_dram = nc.dram_tensor("routed_dram", (2 * TOK + PADS, E), f32, kind="Internal").ap()
    routed_v = routed_dram[0:2 * TOK, :].rearrange("(b p t) f -> b p (t f)", b=B, p=P)
    keep_dram = nc.dram_tensor("keep_dram", (B, P, KEEP), f32, kind="Internal").ap()

    ctx = ExitStack()
    with ctx:
        def sb(name, shape, dt=f32):
            return ctx.enter_context(nc.sbuf_tensor(name, shape, dt))

        def pb(name):
            return ctx.enter_context(nc.psum_tensor(name, [P, 512], f32))

        def sem(name):
            return ctx.enter_context(nc.semaphore(name))

        wqkv = sb("wqkv", [P, 3 * E])
        wgu = sb("wgu", [P, NE, 2 * INTER])
        wdn = sb("wdn", [P, NE, IC * E])
        swgu = sb("swgu", [P, 2 * INTER])
        swdn = sb("swdn", [P, IC * E])
        ident = sb("ident", [P, P])
        ones = sb("ones", [P, P])
        ones_bf = sb("ones_bf", [P, 512], bf16)
        tri = sb("tri", [P, P], bf16)
        head_mask = sb("head_mask", [P, HEADS])
        bias3 = sb("bias3", [P, 3 * E])
        bias_bf = sb("bias_bf", [P, 3 * E], bf16)
        bias_part = sb("bias_part", [P, 3 * E], bf16)
        bias_acc = sb("bias_acc", [P, 3 * E])
        gate_t = sb("gate_t", [P, NE])
        gate_s = sb("gate_s", [P, NE])
        gate_c = sb("gate_c", [P, NE])
        gate_b = sb("gate_b", [P, NE])
        ln_sc = sb("ln_sc", [P, 1])
        ln_bi = sb("ln_bi", [P, 1])
        ln_bi_w = sb("ln_bi_w", [P, P])
        minus1 = sb("minus1", [P, 1])
        rank_of = sb("rank_of", [P, NE])
        region = sb("region", [P, NE])
        tok2 = sb("tok2", [P, B * NT])
        lower8 = sb("lower8", [P, NE, NE])
        unit_no = sb("unit_no", [P, UNITS])
        pad_rows = sb("pad_rows", [P, NE, ROW])
        spare_rows = sb("spare_rows", [P, NE, ROW])
        part_no = sb("part_no", [P, NE])

        xin = [sb(f"xin{i}", [P, NT, E]) for i in range(2)]
        keep = [sb(f"keep{i}", [P, KEEP]) for i in range(2)]
        u_row = [sb(f"u_row{i}", [P, NT, ROW]) for i in range(2)]
        slot_i = [sb(f"slot_i{i}", [P, 2 * NT], i32) for i in range(2)]
        xn = sb("xn", [P, NT, E])
        xnT = sb("xnT", [P, S])
        q_e = sb("q_e", [P, 2, 512])
        k_e = sb("k_e", [P, 2, 2, E])
        pqT = sb("pqT", [P, S])
        pk = sb("pk", [P, NT, E])
        v1 = sb("v1", [P, NT, E + 1])
        kvm = sb("kvm", [P, E + HEADS])
        att = sb("att", [P, NT, E])
        zt = sb("zt", [P, 2, 2, HEADS])
        zr = sb("zr", [P, 2, 2, HEADS])
        uT = sb("uT", [P, S])
        st_a = sb("st_a", [P, NT, 6])
        st_1 = sb("st_1", [P, NT, 6])
        mv_a = sb("mv_a", [P, NT, 2])
        mv_u = sb("mv_u", [P, NT, 2])
        mv_1 = sb("mv_1", [P, NT, 2])
        ve = sb("ve", [P, 2 * NT])
        rs = sb("rs", [P, 2 * NT])
        nt_ = sb("nt_", [P, 2 * NT])
        r_a = sb("r_a", [P, NT])
        r_u = sb("r_u", [P, NT])
        r_41 = sb("r_41", [P, 2 * NT])
        lg = sb("lg", [P, NT, NE])
        lg2 = sb("lg2", [P, NT, NE])
        cand = sb("cand", [P, NT, NE])
        oh1 = sb("oh1", [P, NT, NE])
        oh2 = sb("oh2", [P, NT, NE])
        oh_bf = sb("oh_bf", [P, NT, NE], bf16)
        total = sb("total", [P, NE])
        total_new = sb("total_new", [P, NE])
        total_bf = sb("total_bf", [P, NE], bf16)
        m1 = sb("m1", [P, NT])
        m2 = sb("m2", [P, NT])
        i1 = sb("i1", [P, NT])
        i2 = sb("i2", [P, NT])
        r_in = sb("r_in", [P, NT, NE + 1])
        r_exp = sb("r_exp", [P, NT, NE + 1])
        esum = sb("esum", [P, NT])
        den = sb("den", [P, NT])
        wden = sb("wden", [P, NT])
        pos = sb("pos", [P, NT, NE])
        slot_f = sb("slot_f", [P, 2 * NT])
        act_g = sb("act_g", [P, 2, INTER])
        hid = sb("hid", [P, 2, INTER])
        hidT = sb("hidT", [P, 2, INTER])
        xb = [sb(f"xb{i}", [P, ROW]) for i in range(QU)]
        xbT = sb("xbT", [P, 2, P])
        yb = [sb(f"yb{i}", [P, E]) for i in range(QU)]
        yi = [sb(f"yi{i}", [P, 1], i32) for i in range(QU)]
        other = [sb(f"other{i}", [P, 1]) for i in range(QU)]
        yw = [sb(f"yw{i}", [P, 1]) for i in range(QU)]
        cnt = sb("cnt", [P, NE])
        tl_i = sb("tl_i", [P, NE], i32)
        tl_s = sb("tl_s", [P, NE], i32)
        tl = sb("tl", [P, NE])
        tl8 = sb("tl8", [P, NE, NE])
        cum = sb("cum", [P, NE])
        gain = sb("gain", [P, NE])
        past = sb("past", [P, UNITS, NE])
        pk_sum = sb("pk_sum", [P, UNITS])
        pk_i = sb("pk_i", [P, UNITS], i32)
        unit_row = sb("unit_row", [P, UNITS], i32)
        unit_e = sb("unit_e", [P, UNITS], i32)
        unit_ef = sb("unit_ef", [P, UNITS])
        unit_w = sb("unit_w", [P, UNITS], i32)
        pad_f = sb("pad_f", [P, NE])
        pad_i = sb("pad_i", [P, NE], i32)
        cbuf = [sb(f"cbuf{i}", [P, KEEP]) for i in range(4)]
        res = [sb(f"res{i}", [P, NT, E]) for i in range(4)]
        shift = sb("shift", [P, 2 * NT])
        st_c = sb("st_c", [P, 2 * NT, 6])
        mv_c = sb("mv_c", [P, 2 * NT, 2])
        r_c = sb("r_c", [P, 2 * NT])

        bank_t = [pb("bank_t0"), pb("bank_t1")]
        bank_p = [pb("bank_p0"), pb("bank_p1")]
        bank_g = [pb("bank_g0"), pb("bank_g1")]
        bank_h = [pb("bank_h0"), pb("bank_h1")]

        w_loaded, sw_loaded, ew_loaded = sem("w_loaded"), sem("sw_loaded"), sem("ew_loaded")
        x_loaded = [sem("x_loaded0"), sem("x_loaded1")]
        consts = sem("consts")
        spare_in = sem("spare_in")
        setup = sem("setup")
        setup_ps = sem("setup_ps")
        attn_ps, xnT_ps, q_ps, kv_ps, sum_ps = sem("attn_ps"), sem("xnT_ps"), sem("q_ps"), sem("kv_ps"), sem("sum_ps")
        uT_ps, logit_ps, rank_ps = sem("uT_ps"), sem("logit_ps"), sem("rank_ps")
        gu_ps, ht_ps, y_ps, xbT_ps = sem("gu_ps"), sem("ht_ps"), sem("y_ps"), sem("xbT_ps")
        cnt_ps = sem("cnt_ps")
        xnT_sb, q_exp, kv_exp, uT_sb, r_done = sem("xnT_sb"), sem("q_exp"), sem("kv_exp"), sem("uT_sb"), sem("r_done")
        silu, ht_sb, y_sb = sem("silu"), sem("ht_sb"), sem("y_sb")
        out_add = sem("out_add")
        logit_read, rank_read = sem("logit_read"), sem("rank_read")
        dve = sem("dve")
        dve_passed, pool_passed = sem("dve_passed"), sem("pool_passed")
        att_sb, pq_sb, pk_sb, kvm_sb, xn_sb, u_sb = sem("att_sb"), sem("pq_sb"), sem("pk_sb"), sem("kvm_sb"), sem("xn_sb"), sem("u_sb")
        x1_done = sem("x1_done")
        r_ready, oh_ready, slots_ready, keep_ready = sem("r_ready"), sem("oh_ready"), sem("slots_ready"), sem("keep_ready")
        hid_sb, xbT_sb, yi_sb = sem("hid_sb"), sem("xbT_sb"), sem("yi_sb")
        pads_ready, table_ready = sem("pads_ready"), sem("table_ready")
        res_ready = sem("res_ready")
        scattered = [sem("scattered0"), sem("scattered1")]
        kept = [sem("kept0"), sem("kept1")]
        pads_in = sem("pads_in")
        xb_in = [sem(f"xb_in{i}") for i in range(QU)]
        y_out = [sem(f"y_out{i}") for i in range(QU)]
        c_in = [sem(f"c_in{i}") for i in range(4)]
        stored = [sem(f"stored{i}") for i in range(4)]
        y0_in, y1_in = [sem(f"y0_in{i}") for i in range(4)], [sem(f"y1_in{i}") for i in range(4)]

        def of(b, n, k=0):
            return b * n + k

        def is_int(b):
            return isinstance(b, int)

        def schedule(eng, step):
            for s in range(3):
                step(s, s % 2)
            with eng.Fori(0, (B - 4) // 2) as j:
                step(j * 2 + 3, 1)
                step(j * 2 + 4, 0)
            for s in range(B - 1, B + 2):
                step(s, s % 2)

        def has(b):
            return not is_int(b) or 0 <= b < B

        block = ctx.enter_context(nc.Block())

        @block.sync
        def _(sp):
            sp.dma_start(xin[0][:, :, :], x_v[0, :, :]).then_inc(x_loaded[0], 16)
            sp.dma_start(wqkv[:, :], w_qkv).then_inc(w_loaded, 16)
            for i in range(3):
                sp.dma_start(bias3[i:i + 1, :], b_qkv.rearrange("(a n) -> a n", a=1)).then_inc(w_loaded, 16)
            sp.dma_start(gate_t[:, :], gate_w.rearrange("e f -> f e"), allow_slow_non_contiguous=True).then_inc(w_loaded, 16)
            sp.dma_start(ln_sc[:, :], ln_scale.rearrange("(f a) -> f a", a=1)).then_inc(w_loaded, 16)
            sp.dma_start(ln_bi[:, :], ln_bias.rearrange("(f a) -> f a", a=1)).then_inc(w_loaded, 16)
            sp.dma_start(xin[1][:, :, :], x_v[1, :, :]).then_inc(x_loaded[1], 16)
            sp.dma_start(swgu[:, 0:INTER], swg).then_inc(sw_loaded, 16)
            sp.dma_start(swgu[:, INTER:2 * INTER], swu).then_inc(sw_loaded, 16)
            sp.dma_start(swdn[:, :].rearrange("p (c n) -> p c n", c=IC), swd.rearrange("(c p) n -> p c n", p=P)).then_inc(sw_loaded, 16)
            sp.dma_start(wgu[:, :, 0:INTER], wg.rearrange("e p n -> p e n")).then_inc(ew_loaded, 16)
            sp.dma_start(wgu[:, :, INTER:2 * INTER], wu.rearrange("e p n -> p e n")).then_inc(ew_loaded, 16)
            for e in range(NE):
                sp.dma_start(wdn[:, e, :].rearrange("p (c n) -> p c n", c=IC), wd[e, :, :].rearrange("(c p) n -> p c n", p=P)).then_inc(ew_loaded, 16)
            sp.wait_ge(consts, 1)
            sp.dma_start(slots_dram[NE * CAP:SLOTS, :].rearrange("(p e) n -> p (e n)", p=P),
                         spare_rows[:, :, :].rearrange("p e n -> p (e n)")).then_inc(spare_in, 16)

            def step(s, par):
                if has(s - 1) and has(s) and has(s + 1):
                    sp.wait_ge(x1_done, s)
                    sp.dma_start(xin[1 - par][:, :, :], x_v[ds(s + 1, 1), :, :].rearrange("b p (t n) -> (b p) t n", t=NT)).then_inc(x_loaded[1 - par], 16)
                if has(s - 2):
                    m = s - 2
                    sp.wait_ge(keep_ready, of(m, 1, 1))
                    sp.wait_ge(y_sb, of(m, NT, NT))
                    sp.dma_start(keep_dram[ds(m, 1), :, :].rearrange("b p n -> (b p) n"), keep[par][:, :]).then_inc(kept[par], 16)

            schedule(sp, step)

            sp.wait_ge(table_ready, 1)
            sp.wait_ge(pads_in, 16 * NE)
            sp.wait_ge(spare_in, 16)
            for i in range(2):
                sp.wait_ge(scattered[i], 16 * 2 * NT * (B // 2))

            def load_unit(n, i):
                row = sp.value_load(unit_row[0:1, ds(n, 1)], min_val=0, max_val=SLOTS - P)
                sp.dma_start(xb[i][:, :], slots_dram[ds(row, P), :]).then_inc(xb_in[i], 16)

            for i in range(QU):
                load_unit(i, i)
            with sp.Fori(1, UNITS // QU) as j:
                for i in range(QU):
                    sp.wait_ge(xbT_ps, of(j, QU, i - QU + 1))
                    sp.wait_ge(yi_sb, of(j, QU, i - QU + 1))
                    load_unit(j * QU + i, i)

            for i in range(2):
                sp.wait_ge(kept[i], 16 * (B // 2))

            def load_c(b, i):
                sp.dma_start(cbuf[i][:, :], keep_dram[ds(b, 1), :, :].rearrange("b p n -> (b p) n")).then_inc(c_in[i], 16)

            def store_c(b, i):
                sp.wait_ge(out_add, of(b, NT, NT))
                sp.dma_start(out_v[ds(b, 1), :, :].rearrange("b p n -> (b p) n"), res[i][:, :, :].rearrange("p t n -> p (t n)")).then_inc(stored[i], 16)

            for i in range(4):
                load_c(i, i)
            for i in range(4):
                store_c(i, i)
                load_c(i + 4, i)
            for i in range(4):
                store_c(i + 4, i)
            for i in range(4):
                sp.wait_ge(stored[i], 16 * (B // 4))

        @block.gpsimd
        def _(pool):
            g = nc.gpsimd
            n = [0]

            def link(ins):
                n[0] += 1
                ins.then_inc(setup, 1)

            link(g.memset(ident[:, :], 0.0))
            link(g.memset(ones[:, :], 1.0))
            link(g.memset(ones_bf[:, :], 1.0))
            link(g.memset(tri[:, :], 1.0))
            link(g.memset(head_mask[:, :], 1.0))
            link(g.memset(lower8[:, :, :], 1.0))
            link(g.memset(spare_rows[:, :, :], 0.0))
            link(g.memset(pad_rows[:, :, :], 0.0))
            link(g.memset(v1[:, :, E:E + 1], 1.0))
            link(g.memset(total[:, :], 0.0))
            link(g.memset(total_bf[:, :], 0.0))
            link(g.iota(rank_of[:, :], [[-1, NE]], base=NE, channel_multiplier=0, allow_small_or_imprecise_dtypes=True))
            for e in range(NE):
                link(g.memset(region[:, e:e + 1], float(e * CAP)))
            link(g.iota(tok2[:, :].rearrange("p (b t) -> p b t", b=B), [[2 * S, B], [2, NT]], base=0, channel_multiplier=2 * NT, allow_small_or_imprecise_dtypes=True))
            link(g.iota(unit_no[:, :], [[1, UNITS]], base=0, channel_multiplier=0, allow_small_or_imprecise_dtypes=True))
            link(g.iota(part_no[:, :], [[0, NE]], base=0, channel_multiplier=1, allow_small_or_imprecise_dtypes=True))
            pool.wait_ge(setup, n[0])
            link(g.affine_select(out=ident[:, :], in_=ident[:, :], compare_op=ALU.not_equal, fill=1.0, base=0, pattern=[[-1, P]], channel_multiplier=1))
            link(g.affine_select(out=tri[:, :], in_=tri[:, :], compare_op=ALU.is_gt, fill=0.0, base=0, pattern=[[1, P]], channel_multiplier=-1))
            link(g.affine_select(out=lower8[:, :, :], in_=lower8[:, :, :], compare_op=ALU.is_ge, fill=0.0, base=0, pattern=[[1, NE], [-1, NE]], channel_multiplier=0))
            link(g.affine_select(out=head_mask[:, :], in_=head_mask[:, :], compare_op=ALU.is_ge, fill=0.0, base=0, pattern=[[-D, HEADS]], channel_multiplier=1))
            link(g.iota(pad_rows[:, :, E:E + 1], [[2 * P, NE], [0, 1]], base=2 * TOK, channel_multiplier=2, allow_small_or_imprecise_dtypes=True))
            link(g.iota(spare_rows[:, :, E:E + 1], [[2, NE], [0, 1]], base=2 * TOK + 2 * NE * P, channel_multiplier=2 * NE, allow_small_or_imprecise_dtypes=True))
            pool.wait_ge(setup, n[0])
            g.affine_select(out=head_mask[:, :], in_=head_mask[:, :], compare_op=ALU.is_ge, fill=0.0, base=D - 1, pattern=[[D, HEADS]], channel_multiplier=-1).then_inc(consts, 1)

            def scatter(k, par):
                pool.wait_ge(slots_ready, of(k, 1, 1))
                pool.sem_inc(pool_passed, 1)
                for t in range(NT):
                    for c in range(2):
                        g.indirect_dma_start(slots_dram, bass.IndirectOffsetOnAxis(ap=slot_i[par][:, c * NT + t:c * NT + t + 1], axis=0),
                                             u_row[par][:, t, :], None).then_inc(scattered[par], 16)

            with pool.Fori(0, B // 2) as j:
                scatter(j * 2, 0)
                scatter(j * 2 + 1, 1)
            pool.wait_ge(pads_ready, 1)
            for e in range(NE):
                g.indirect_dma_start(slots_dram, bass.IndirectOffsetOnAxis(ap=pad_i[:, e:e + 1], axis=0), pad_rows[:, e, :], None).then_inc(pads_in, 16)

            def scatter_y(n_, i):
                pool.wait_ge(y_sb, n_ + TOK // P + 1)
                pool.wait_ge(yi_sb, n_ + 1)
                pool.sem_inc(pool_passed, 1)
                g.indirect_dma_start(routed_dram, bass.IndirectOffsetOnAxis(ap=yi[i][:, 0:1], axis=0), yb[i][:, :], None).then_inc(y_out[i], 16)

            with pool.Fori(0, UNITS // QU) as j:
                for i in range(QU):
                    scatter_y(j * QU + i, i)

            for i in range(QU):
                pool.wait_ge(y_out[i], 16 * (UNITS // QU))

            def add_rows(b, i, c, after, in_):
                pool.wait_ge(after, (b - i) * 4 + 16)
                pool.dma_start(cbuf[i][:, NT * E:2 * NT * E].rearrange("p (t n) -> p t n", n=E), routed_v[ds(b, 1), :, :].rearrange("b p (t c n) -> (b p) t c n", c=2, n=E)[:, :, c, :],
                               accum_op=ALU.add).then_inc(in_, 16)

            with pool.Fori(0, B // 4) as j:
                for i in range(4):
                    add_rows(j * 4 + i, i, 0, c_in[i], y0_in[i])
                for i in range(4):
                    add_rows(j * 4 + i, i, 1, y0_in[i], y1_in[i])

        @block.tensor
        def _(pe):
            mm = nc.tensor.matmul
            pe.wait_ge(consts, 1)
            pe.wait_ge(setup_ps, 1)
            mm(bank_h[0][:, 0:NE], ones[:, :], gate_s[:, :], start=True, stop=True)
            mm(bank_h[0][:, NE:2 * NE], ln_bi_w[:, :], gate_t[:, :], start=True, stop=True).then_inc(setup_ps, 1)

            def attn(k, uses):
                pe.wait_ge(kvm_sb, of(k, 1, 1))
                pe.wait_ge(pq_sb, of(k, 2, 2))
                for i in uses:
                    if i < 2:
                        pe.wait_ge(pk_sb, of(k, 4, 4))
                    else:
                        pe.wait_ge(att_sb, of(k, 4, i - 1))
                    for h in range(2):
                        t = 2 * i + h
                        last = mm(bank_p[i % 2][:, 256 * h:256 * h + E + HEADS], pqT[:, t * P:(t + 1) * P], kvm[:, :], start=True, stop=True)
                    last.then_inc(attn_ps, 1)

            def front(f):
                pe.wait_ge(xn_sb, of(f, 1, 1))
                for i in range(2):
                    if has(f - 2):
                        if i == 0:
                            pe.wait_ge(uT_sb, of(f, 2, -3))
                        else:
                            pe.wait_ge(logit_read, f - 1)
                    elif has(f - 1):
                        if i == 0:
                            pe.wait_ge(kvm_sb, f)
                        else:
                            pe.wait_ge(xnT_sb, 2 * f)
                    for t in range(4 * i, 4 * i + 4):
                        last = nc.tensor.transpose(bank_t[i][:, (t % 4) * P:(t % 4 + 1) * P], xn[:, t, :], ident[:, :])
                    last.then_inc(xnT_ps, 1)
                for i in range(2):
                    pe.wait_ge(xnT_sb, of(f, 2, i + 1))
                    if not is_int(f) or f > 0:
                        pe.wait_ge(att_sb, of(f, 4, i - 1))
                    mm(bank_p[i][:, :], bias_bf[:, 0:E], ones_bf[:, :], start=True, stop=False)
                    mm(bank_p[i][:, :], wqkv[:, 0:E], xnT[:, i * 512:(i + 1) * 512], start=False, stop=True).then_inc(q_ps, 1)
                for i in range(4):
                    if i < 2:
                        pe.wait_ge(pq_sb, of(f, 2, i + 1))
                    else:
                        pe.wait_ge(pk_sb, of(f, 4, i - 1))
                    for h in range(2):
                        t = 2 * i + h
                        o = bank_p[i % 2][:, 256 * h:256 * h + 256]
                        mm(o, ones_bf[:, 0:P], bias_bf[:, E:3 * E], start=True, stop=False)
                        last = mm(o, xnT[:, t * P:(t + 1) * P], wqkv[:, E:3 * E], start=False, stop=True)
                    last.then_inc(kv_ps, 1)
                for t in range(NT):
                    if t % 2 == 0:
                        pe.wait_ge(pk_sb, of(f, 4, t // 2 + 1))
                    last = mm(bank_t[0][:, 0:E + 1], pk[:, t, :], v1[:, t, :], start=t == 0, stop=t == NT - 1)
                last.then_inc(sum_ps, 1)

            def gate_up(n_, i, xT, w):
                if not is_int(n_) or n_ >= 2:
                    pe.wait_ge(hid_sb, n_ - 1)
                mm(bank_g[i][:, :], xT, w, start=True, stop=True).then_inc(gu_ps, 1)

            def hid_t(n_, i):
                pe.wait_ge(hid_sb, n_ + 1)
                if not is_int(n_) or n_ >= 2:
                    pe.wait_ge(ht_sb, n_ - 1)
                for c in range(IC):
                    last = nc.tensor.transpose(bank_h[i][:, c * P:(c + 1) * P], hid[:, i, c * P:(c + 1) * P], ident[:, :])
                last.then_inc(ht_ps, 1)

            def down(n_, i, w):
                pe.wait_ge(ht_sb, n_ + 1)
                if not is_int(n_) or n_ >= 2:
                    pe.wait_ge(y_sb, n_ - 1)
                for c in range(IC):
                    last = mm(bank_h[i][:, INTER:INTER + E], hidT[:, i, c * P:(c + 1) * P], w(c), start=c == 0, stop=c == IC - 1)
                last.then_inc(y_ps, 1)

            def middle_u(k, par):
                for i in range(2):
                    pe.wait_ge(u_sb, of(k, 2, i + 1))
                    if i == 0:
                        if has(k + 1):
                            pe.wait_ge(kvm_sb, of(k, 1, 2))
                    elif has(k - 1):
                        pe.wait_ge(rank_read, k)
                    else:
                        pe.wait_ge(xnT_sb, of(k, 2, 4))
                    for t in range(4 * i, 4 * i + 4):
                        last = nc.tensor.transpose(bank_t[i][:, (t % 4) * P:(t % 4 + 1) * P], u_row[par][:, t, 0:E], ident[:, :])
                    last.then_inc(uT_ps, 1)
                pe.wait_ge(uT_sb, of(k, 2, 2))
                for t in range(NT):
                    last = mm(bank_t[1][:, t * NE:(t + 1) * NE], uT[:, t * P:(t + 1) * P], gate_c[:, :], start=True, stop=True)
                last.then_inc(logit_ps, 1)

            def end(m):
                for t in range(NT + 2):
                    n_ = m * NT + t
                    if t < NT:
                        gate_up(n_, t % 2, uT[:, t * P:(t + 1) * P], swgu[:, :])
                    if t >= 2:
                        down(n_ - 2, t % 2, lambda c: swdn[:, c * E:(c + 1) * E])
                    if 1 <= t <= NT:
                        hid_t(n_ - 1, (t - 1) % 2)
                    if t == 3:
                        pe.wait_ge(oh_ready, of(m, 1, 1))
                        o = bank_t[1]
                        oh = oh_bf[:, :, :].rearrange("p t e -> p (t e)")
                        mm(o[:, 64:128], tri[:, :], oh, start=True, stop=False)
                        for s in range(1, NT):
                            mm(o[:, 64 + s * NE:128], ones_bf[:, 0:P], oh[:, 0:(NT - s) * NE], start=False, stop=False)
                        mm(o[:, 64:128], ones_bf[:, 0:P], total_bf[:, :].unsqueeze(1).to_broadcast([P, NT, NE]), start=False, stop=True).then_inc(rank_ps, 1)

            def step(s, par):
                if has(s - 1):
                    attn(s - 1, range(4))
                if has(s):
                    front(s)
                if has(s - 2):
                    end(s - 2)
                if has(s - 1):
                    middle_u(s - 1, 1 - par)

            pe.wait_ge(setup_ps, 3)
            pe.wait_ge(w_loaded, 16 * 7)
            pe.wait_ge(sw_loaded, 16 * 3)
            schedule(pe, step)

            pe.wait_ge(oh_ready, B + 1)
            mm(bank_t[0][:, 0:NE], ones_bf[:, 0:P], total_bf[:, :], start=True, stop=True).then_inc(cnt_ps, 1)

            N0 = TOK // P
            pe.wait_ge(ew_loaded, 16 * (2 + NE))
            pe.wait_ge(table_ready, 1)

            def expert(n_):
                return pe.value_load(unit_e[0:1, ds(n_, 1)], min_val=0, max_val=NE - 1)

            def routed_down(n_, i, e):
                down(n_ + N0, i, lambda c: wdn[:, ds(e, 1), c * E:(c + 1) * E].rearrange("p e n -> p (e n)"))

            def group(j, first, final):
                e = {0: expert(j * QU)}
                for i in range(QU):
                    n_ = j * QU + i
                    pe.wait_ge(xbT_sb, n_ + 1)
                    pe.wait_ge(hid_sb, n_ + N0 - 1)
                    mm(bank_g[i % 2][:, :], xbT[:, i % 2, :], wgu[:, ds(e[i], 1), :].rearrange("p e n -> p (e n)"), start=True, stop=True).then_inc(gu_ps, 1)
                    if i < QU - 1:
                        e[i + 1] = expert(j * QU + (i + 1))
                    if not first and i < 2:
                        e[i - 2] = expert(j * QU + (i - 2))
                    if not (final and i == QU - 1):
                        nx = (i + 1) % QU
                        pe.wait_ge(xb_in[nx], (j + (i + 1) // QU) * 16 + 16)
                        if not first or i >= 1:
                            pe.wait_ge(xbT_sb, n_)
                        nc.tensor.transpose(bank_t[nx % 2][:, 0:E], xb[nx][:, 0:E], ident[:, :]).then_inc(xbT_ps, 1)
                    if not first or i >= 2:
                        routed_down(n_ - 2, i % 2, e[i - 2])
                    if not first or i >= 1:
                        hid_t(n_ + N0 - 1, (i + 1) % 2)
                return e

            pe.wait_ge(xb_in[0], 16)
            nc.tensor.transpose(bank_t[0][:, 0:E], xb[0][:, 0:E], ident[:, :]).then_inc(xbT_ps, 1)
            NJ = UNITS // QU
            group(0, True, False)
            with pe.Fori(1, NJ - 1) as j:
                group(j, False, False)
            e = group(NJ - 1, False, True)
            routed_down(UNITS - 2, UNITS % 2, e[QU - 2])
            hid_t(UNITS - 1 + N0, (UNITS - 1) % 2)
            routed_down(UNITS - 1, (UNITS - 1) % 2, e[QU - 1])

        @block.scalar
        def _(act):
            A = nc.scalar.activation

            def front(f):
                for i in range(2):
                    act.wait_ge(xnT_ps, of(f, 2, i + 1))
                    A(xnT[:, i * 512:(i + 1) * 512], bank_t[i][:, :], ACT.Copy).then_inc(xnT_sb, 1)
                for i in range(2):
                    act.wait_ge(q_ps, of(f, 2, i + 1))
                    A(q_e[:, i, :], bank_p[i][:, :], ACT.Exp, bias=minus1[:, 0:1]).then_inc(q_exp, 1)
                for i in range(4):
                    act.wait_ge(kv_ps, of(f, 4, i + 1))
                    o = bank_p[i % 2][:, :].rearrange("p (h n) -> p h n", h=2)
                    A(v1[:, 2 * i:2 * i + 2, 0:E], o[:, :, E:2 * E], ACT.Copy)
                    A(k_e[:, i % 2, :, :], o[:, :, 0:E], ACT.Exp, bias=minus1[:, 0:1]).then_inc(kv_exp, 1)

            def silu_of(n_, i):
                act.wait_ge(gu_ps, n_ + 1)
                A(act_g[:, i, :], bank_g[i][:, 0:INTER], ACT.Silu).then_inc(silu, 1)

            def ht_of(n_, i):
                act.wait_ge(ht_ps, n_ + 1)
                A(hidT[:, i, :], bank_h[i][:, 0:INTER], ACT.Copy).then_inc(ht_sb, 1)

            def step(s, par):
                if has(s):
                    front(s)
                if has(s - 2):
                    m = s - 2
                    act.wait_ge(r_ready, of(m, 1, 1))
                    A(r_exp[:, :, :], r_in[:, :, :], ACT.Exp).then_inc(r_done, 1)
                    for t in range(NT + 2):
                        n_ = m * NT + t
                        if t < NT:
                            silu_of(n_, t % 2)
                        if t >= 2:
                            act.wait_ge(y_ps, n_ - 1)
                            A(keep[par][:, (NT + t - 2) * E:(NT + t - 1) * E], bank_h[t % 2][:, INTER:INTER + E], ACT.Copy).then_inc(y_sb, 1)
                        if 1 <= t <= NT:
                            ht_of(n_ - 1, (t - 1) % 2)
                if has(s - 1):
                    for i in range(2):
                        act.wait_ge(uT_ps, of(s - 1, 2, i + 1))
                        A(uT[:, i * 512:(i + 1) * 512], bank_t[i][:, :], ACT.Copy).then_inc(uT_sb, 1)

            act.wait_ge(setup_ps, 3)
            schedule(act, step)

            N0 = TOK // P

            def unit(j, i, first):
                n_ = j * QU + i
                silu_of(n_ + N0, i % 2)
                if not first or i >= 2:
                    y_of(n_ - 2, (i - 2) % QU, j, first)
                if not first or i >= 1:
                    ht_of(n_ + N0 - 1, (i - 1) % 2)

            def y_of(n_, i, j, first):
                act.wait_ge(y_ps, n_ + N0 + 1)
                if not first:
                    act.wait_ge(y_out[i], (j - (1 if i >= QU - 2 else 0)) * 16)
                A(yb[i][:, :], bank_h[i % 2][:, INTER:INTER + E], ACT.Copy, scale=yw[i][:, 0:1]).then_inc(y_sb, 1)

            for i in range(QU):
                unit(0, i, True)
            for i in range(QU):
                n_ = QU + i
                silu_of(n_ + N0, i % 2)
                y_of(n_ - 2, (i - 2) % QU, 1, i < 2)
                ht_of(n_ + N0 - 1, (i - 1) % 2)
            with act.Fori(2, UNITS // QU) as j:
                for i in range(QU):
                    unit(j, i, False)
            y_of(UNITS - 2, (UNITS - 2) % QU, UNITS // QU, False)
            ht_of(UNITS - 1 + N0, (UNITS - 1) % 2)
            y_of(UNITS - 1, (UNITS - 1) % QU, UNITS // QU, False)

            def final(b, i):
                for t in range(NT):
                    act.wait_ge(res_ready, of(b, NT, t + 1))
                    A(res[i][:, t, :], res[i][:, t, :], ACT.Identity, bias=shift[:, (i % 2) * NT + t:(i % 2) * NT + t + 1]).then_inc(out_add, 1)

            with act.Fori(0, B // 4) as j:
                for i in range(4):
                    final(j * 4 + i, i)

        @block.vector
        def _(dv):
            v = nc.vector
            base, n = [0], [0]

            def inc(ins):
                n[0] += 1
                ins.then_inc(dve, 1)
                return n[0]

            def wait(k=None):
                dv.wait_ge(dve, base[0] + (n[0] if k is None else k))

            def link(ins):
                inc(ins)
                wait()

            def rsqrt(dst, var, t):
                k = inc(v.tensor_scalar(dst.bitcast(i32), var.bitcast(i32), -0.5, float(0x5f3759df), ALU.mult, ALU.add))
                yield
                for _ in range(3):
                    wait(k)
                    k = inc(v.tensor_tensor(t, dst, dst, ALU.mult))
                    yield
                    wait(k)
                    k = inc(v.scalar_tensor_tensor(out=t, in0=t, scalar=-0.5, in1=var, op0=ALU.mult, op1=ALU.mult))
                    yield
                    wait(k)
                    k = inc(v.scalar_tensor_tensor(out=dst, in0=t, scalar=1.5, in1=dst, op0=ALU.add, op1=ALU.mult))
                    yield
                wait(k)

            def stats(src, st, mv, ve, tiles=NT):
                for t in range(tiles):
                    k = inc(v.bn_stats(st[:, t, :], src(t)))
                    yield
                wait(k)
                dv.sem_inc(dve_passed, 1)
                for t in range(tiles):
                    k = inc(v.bn_aggr(mv[:, t, :], st[:, t, :]))
                    yield
                wait(k)
                k = inc(v.tensor_scalar(ve, mv[:, :, 1], LN_EPS, None, ALU.add))
                yield
                wait(k)

            minus_one = v.memset(minus1[:, :], -1.0)
            inc(minus_one)
            link(v.memset(bias_acc[:, :], 0.0))
            link(v.memset(bias_bf[:, :], 0.0))
            dv.wait_ge(consts, 1)
            dv.wait_ge(w_loaded, 16 * 7)
            link(v.tensor_scalar(bias3[0:3, 0:2 * E], bias3[0:3, 0:2 * E], 1.0, None, ALU.add))
            for i in range(3):
                link(v.tensor_copy(bias_part[0:3, :], bias3[0:3, :]))
                link(v.scalar_tensor_tensor(out=bias_acc[0:3, :], in0=bias_part[0:3, :], scalar=ident[0:3, i:i + 1], in1=bias_acc[0:3, :], op0=ALU.mult, op1=ALU.add))
                if i < 2:
                    link(v.tensor_tensor(bias3[0:3, :], bias3[0:3, :], bias_part[0:3, :], ALU.subtract))
            link(v.tensor_copy(bias_bf[0:3, :], bias_acc[0:3, :]))
            v.tensor_scalar(gate_s[:, :], gate_t[:, :], ln_sc[:, 0:1], None, ALU.mult)
            v.tensor_scalar(ln_bi_w[:, :], ones[:, :], ln_bi[:, 0:1], None, ALU.mult).then_inc(setup_ps, 1)
            dv.wait_ge(setup_ps, 2)
            v.tensor_copy(gate_b[:, :], bank_h[0][:, NE:2 * NE])
            v.scalar_tensor_tensor(out=gate_c[:, :], in0=bank_h[0][:, 0:NE], scalar=-1.0 / E, in1=gate_s[:, :], op0=ALU.mult, op1=ALU.add).then_inc(setup_ps, 1)

            def phi(f):
                for i in range(2):
                    dv.wait_ge(q_exp, of(f, 2, i + 1))
                    v.scalar_tensor_tensor(out=pqT[:, i * 512:(i + 1) * 512], in0=q_e[:, i, :], scalar=1.0, in1=bank_p[i][:, :],
                                           op0=ALU.min, op1=ALU.max).then_inc(pq_sb, 1)
                    yield
                for i in range(4):
                    dv.wait_ge(kv_exp, of(f, 4, i + 1))
                    v.scalar_tensor_tensor(out=pk[:, 2 * i:2 * i + 2, :], in0=k_e[:, i % 2, :, :], scalar=1.0,
                                           in1=bank_p[i % 2][:, :].rearrange("p (h n) -> p h n", h=2)[:, :, 0:E],
                                           op0=ALU.min, op1=ALU.max).then_inc(pk_sb, 1)
                    yield
                dv.wait_ge(sum_ps, of(f, 1, 1))
                v.tensor_tensor(kvm[:, 0:E].rearrange("p (h m) -> p h m", m=D), bank_t[0][:, 0:E].rearrange("p (h m) -> p h m", m=D),
                                head_mask[:, :].unsqueeze(2).to_broadcast([P, HEADS, D]), ALU.mult)
                v.tensor_scalar(kvm[:, E:E + HEADS], head_mask[:, :], bank_t[0][:, E:E + 1], None, ALU.mult).then_inc(kvm_sb, 1)
                yield

            def hidden(n_, i):
                dv.wait_ge(silu, n_ + 1)
                v.tensor_tensor(hid[:, i, :], act_g[:, i, :], bank_g[i][:, INTER:2 * INTER], ALU.mult).then_inc(hid_sb, 1)

            def products(m):
                for t in range(NT):
                    hidden(m * NT + t, t % 2)
                    yield

            def attention(k, par):
                kp = keep[par]
                x1 = kp[:, 0:NT * E].rearrange("p (t n) -> p t n", n=E)
                for i in range(4):
                    dv.wait_ge(attn_ps, of(k, 4, i + 1))
                    a = bank_p[i % 2][:, :].rearrange("p (h n) -> p h n", h=2)
                    c = inc(v.tensor_scalar(zt[:, i % 2, :, :], a[:, :, E:E + HEADS], 1e-6, None, ALU.add))
                    yield
                    wait(c)
                    c = inc(v.reciprocal(zr[:, i % 2, :, :], zt[:, i % 2, :, :]))
                    yield
                    wait(c)
                    for h in range(2):
                        last = v.tensor_tensor(att[:, 2 * i + h, :].rearrange("p (h m) -> p h m", m=D), a[:, h, 0:E].rearrange("p (h m) -> p h m", m=D),
                                               zr[:, i % 2, h, :].unsqueeze(2).to_broadcast([P, HEADS, D]), ALU.mult)
                    last.then_inc(att_sb, 1)
                    yield
                dv.wait_ge(att_sb, of(k, 4, 4))
                yield from stats(lambda t: att[:, t, :], st_a, mv_a, ve[:, 0:NT])
                yield from rsqrt(r_a[:, :], ve[:, 0:NT], nt_[:, 0:NT])
                if not is_int(k) or k >= 2:
                    dv.wait_ge(kept[par], (k - par) * 8)
                for t in range(NT):
                    last = v.scalar_tensor_tensor(out=x1[:, t, :], in0=att[:, t, :], scalar=r_a[:, t:t + 1], in1=xin[par][:, t, :], op0=ALU.mult, op1=ALU.add)
                    if t < NT - 1:
                        yield
                last.then_inc(x1_done, 1)
                v.scalar_tensor_tensor(out=kp[:, 2 * NT * E:2 * NT * E + NT], in0=mv_a[:, :, 0], scalar=-1.0, in1=r_a[:, :], op0=ALU.mult, op1=ALU.mult).then_inc(keep_ready, 1)
                yield
                dv.wait_ge(x1_done, of(k, 1, 1))
                yield from stats(lambda t: x1[:, t, :], st_a, mv_u, ve[:, 0:NT])
                yield from rsqrt(r_u[:, :], ve[:, 0:NT], nt_[:, 0:NT])
                if not is_int(k) or k >= 2:
                    dv.wait_ge(scattered[par], (k - par) * (8 * 2 * NT))
                for t in range(NT):
                    last = v.tensor_scalar(u_row[par][:, t, 0:E], x1[:, t, :], mv_u[:, t, 0:1], r_u[:, t:t + 1], ALU.subtract, ALU.mult)
                    if t % 4 == 3:
                        last.then_inc(u_sb, 1)
                    yield
                c = inc(v.tensor_tensor(ve[:, 0:NT], mv_u[:, :, 1], r_u[:, :], ALU.mult))
                yield
                wait(c)
                c = inc(v.tensor_tensor(ve[:, 0:NT], ve[:, 0:NT], r_u[:, :], ALU.mult))
                yield
                wait(c)
                c = inc(v.tensor_scalar(ve[:, 0:NT], ve[:, 0:NT], LN_EPS, None, ALU.add))
                yield
                wait(c)

            def norm_x(f, par):
                dv.wait_ge(x_loaded[par], (f - par) * 8 + 16)
                yield from stats(lambda t: xin[par][:, t, :], st_1, mv_1, ve[:, NT:2 * NT])

            def apply_x(par):
                for t in range(NT):
                    last = v.tensor_scalar(xn[:, t, :], xin[par][:, t, :], mv_1[:, t, 0:1], r_41[:, NT + t:NT + t + 1], ALU.subtract, ALU.mult)
                    if t < NT - 1:
                        yield
                last.then_inc(xn_sb, 1)
                yield

            def bc(a):
                return a.unsqueeze(2).to_broadcast([P, NT, NE])

            def per_e(a):
                return a.unsqueeze(1).to_broadcast([P, NT, NE])

            total_at = [0]

            def router(m, par):
                dv.wait_ge(logit_ps, of(m, 1, 1))
                c = inc(v.tensor_tensor(lg[:, :, :], bank_t[1][:, 0:NT * NE].rearrange("p (t e) -> p t e", e=NE), bc(r_41[:, 0:NT]), ALU.mult))
                yield
                wait(c)
                v.tensor_tensor(lg[:, :, :], lg[:, :, :], per_e(gate_b[:, :]), ALU.add).then_inc(logit_read, 1)
                yield
                dv.wait_ge(logit_read, of(m, 1, 1))
                c = inc(v.tensor_reduce(m1[:, :], lg[:, :, :], AX.X, ALU.max))
                yield
                wait(c)
                c = inc(v.tensor_tensor(cand[:, :, :], lg[:, :, :], bc(m1[:, :]), ALU.is_equal))
                yield
                wait(c)
                c = inc(v.tensor_tensor(cand[:, :, :], cand[:, :, :], per_e(rank_of[:, :]), ALU.mult))
                yield
                wait(c)
                c = inc(v.tensor_reduce(i1[:, :], cand[:, :, :], AX.X, ALU.max))
                yield
                wait(c)
                c = inc(v.tensor_tensor(oh1[:, :, :], per_e(rank_of[:, :]), bc(i1[:, :]), ALU.is_equal))
                yield
                wait(c)
                c = inc(v.scalar_tensor_tensor(out=lg2[:, :, :], in0=oh1[:, :, :], scalar=-3e38, in1=lg[:, :, :], op0=ALU.mult, op1=ALU.add))
                yield
                wait(c)
                c = inc(v.tensor_reduce(m2[:, :], lg2[:, :, :], AX.X, ALU.max))
                yield
                wait(c)
                v.tensor_tensor(r_in[:, :, 0:NE], lg[:, :, :], bc(m1[:, :]), ALU.subtract)
                v.tensor_tensor(r_in[:, :, NE], m2[:, :], m1[:, :], ALU.subtract).then_inc(r_ready, 1)
                yield
                c = inc(v.tensor_tensor(cand[:, :, :], lg2[:, :, :], bc(m2[:, :]), ALU.is_equal))
                yield
                wait(c)
                c = inc(v.tensor_tensor(cand[:, :, :], cand[:, :, :], per_e(rank_of[:, :]), ALU.mult))
                yield
                wait(c)
                c = inc(v.tensor_reduce(i2[:, :], cand[:, :, :], AX.X, ALU.max))
                yield
                wait(c)
                c = inc(v.tensor_tensor(oh2[:, :, :], per_e(rank_of[:, :]), bc(i2[:, :]), ALU.is_equal))
                yield
                wait(c)
                v.tensor_tensor(oh_bf[:, :, :], oh1[:, :, :], oh2[:, :, :], ALU.add).then_inc(oh_ready, 1)
                yield
                v.tensor_scalar(u_row[par][:, :, E + 1], i1[:, :], -1.0, float(NE), ALU.mult, ALU.add)
                v.tensor_copy(u_row[par][:, :, E], tok2[:, ds(m * NT, NT)])
                yield
                dv.wait_ge(oh_ready, of(m, 1, 1))
                total_at[0] = inc(v.tensor_reduce(total_new[:, :], oh_bf[:, :, :].rearrange("p t e -> p e t"), AX.X, ALU.add))
                yield

            def dispatch(m, par):
                dv.wait_ge(r_done, of(m, 1, 1))
                c = inc(v.tensor_reduce(esum[:, :], r_exp[:, :, 0:NE], AX.X, ALU.add))
                yield
                wait(c)
                c = inc(v.scalar_tensor_tensor(out=den[:, :], in0=esum[:, :], scalar=EPS, in1=r_exp[:, :, NE], op0=ALU.mult, op1=ALU.add))
                yield
                wait(c)
                c = inc(v.tensor_scalar(den[:, :], den[:, :], 1.0, None, ALU.add))
                yield
                wait(c)
                c = inc(v.reciprocal(wden[:, :], den[:, :]))
                yield
                wait(c)
                v.tensor_copy(u_row[par][:, :, E + 2], wden[:, :])
                v.scalar_tensor_tensor(out=u_row[par][:, :, E + 3], in0=r_exp[:, :, NE], scalar=-1.0, in1=wden[:, :], op0=ALU.add, op1=ALU.mult)
                yield
                dv.wait_ge(rank_ps, of(m, 1, 1))
                wait(total_at[0])
                v.tensor_tensor(pos[:, :, :], bank_t[1][:, 64:128].rearrange("p (t e) -> p t e", e=NE), per_e(region[:, :]), ALU.add).then_inc(rank_read, 1)
                c = inc(v.tensor_tensor(total[:, :], total[:, :], total_new[:, :], ALU.add))
                yield
                wait(c)
                inc(v.tensor_copy(total_bf[:, :], total[:, :]))
                inc(v.tensor_tensor(oh1[:, :, :], oh1[:, :, :], pos[:, :, :], ALU.mult))
                c = inc(v.tensor_tensor(oh2[:, :, :], oh2[:, :, :], pos[:, :, :], ALU.mult))
                yield
                wait(c)
                inc(v.tensor_reduce(slot_f[:, 0:NT], oh1[:, :, :], AX.X, ALU.add))
                c = inc(v.tensor_reduce(slot_f[:, NT:2 * NT], oh2[:, :, :], AX.X, ALU.add))
                yield
                wait(c)
                v.tensor_copy(slot_i[par][:, :], slot_f[:, :]).then_inc(slots_ready, 1)
                yield

            def main(s, par):
                if has(s - 1):
                    yield from attention(s - 1, 1 - par)
                if has(s + 1):
                    yield from norm_x(s + 1, 1 - par)
                    yield from rsqrt(r_41[:, :], ve[:, :], nt_[:, :])
                    yield from apply_x(1 - par)
                else:
                    yield from rsqrt(r_41[:, 0:NT], ve[:, 0:NT], nt_[:, 0:NT])

            def nothing():
                return iter(())

            def step(s, par):
                m = s - 2
                side = [(phi(s) if has(s) else nothing(), PHI_AT),
                        (router(m, par) if has(m) else nothing(), ROUTER_AT),
                        (products(m) if has(m) else nothing(), PRODUCTS_AT),
                        (dispatch(m, par) if has(m) else nothing(), DISPATCH_AT)]
                if has(s - 1):
                    for i, _ in enumerate(main(s, par)):
                        for strand, at in side:
                            if i in at:
                                next(strand, None)
                for strand, _ in side:
                    for _ in strand:
                        pass

            for f in range(2):
                if f:
                    for _ in phi(0):
                        pass
                for _ in norm_x(f, f):
                    pass
                for _ in rsqrt(r_41[:, NT:2 * NT], ve[:, NT:2 * NT], nt_[:, NT:2 * NT]):
                    pass
                for _ in apply_x(f):
                    pass
            step(1, 1)
            step(2, 0)
            start = base[0] + n[0]
            LOOPS = (B - 4) // 2
            with dv.Fori(0, LOOPS) as j:
                base[0], n[0] = j * DVE_PAIR + start, 0
                step(j * 2 + 3, 1)
                step(j * 2 + 4, 0)
                assert n[0] == DVE_PAIR, f"DVE_PAIR = {n[0]}"
            base[0], n[0] = start + LOOPS * DVE_PAIR, 0
            for s in range(B - 1, B + 2):
                step(s, s % 2)
            dv.wait_ge(slots_ready, B)
            v.tensor_copy(total_bf[:, :], total[:, :]).then_inc(oh_ready, 1)

            dv.wait_ge(cnt_ps, 1)
            link(v.tensor_copy(cnt[:, :], bank_t[0][:, 0:NE]))
            inc(v.tensor_tensor(pad_f[:, :], cnt[:, :], region[:, :], ALU.add))
            link(v.tensor_scalar(tl_i[:, :], cnt[:, :], float(P - 1), None, ALU.add))
            inc(v.tensor_tensor(pad_f[:, :], pad_f[:, :], part_no[:, :], ALU.add))
            link(v.tensor_scalar(tl_s[:, :], tl_i[:, :], 7, None, ALU.arith_shift_right))
            v.tensor_copy(pad_i[:, :], pad_f[:, :]).then_inc(pads_ready, 1)
            link(v.tensor_copy(tl[:, :], tl_s[:, :]))
            inc(v.tensor_scalar(gain[:, :], tl[:, :], float(-P), float(CAP + (1 << SHIFT)), ALU.mult, ALU.add))
            link(v.tensor_tensor(tl8[:, :, :], lower8[:, :, :], tl[:, :].unsqueeze(1).to_broadcast([P, NE, NE]), ALU.mult))
            link(v.tensor_reduce(cum[:, :], tl8[:, :, :], AX.X, ALU.add))
            link(v.tensor_tensor(past[:, :, :], unit_no[:, :].unsqueeze(2).to_broadcast([P, UNITS, NE]),
                                 cum[:, :].unsqueeze(1).to_broadcast([P, UNITS, NE]), ALU.is_ge))
            link(v.tensor_tensor(past[:, :, :], past[:, :, :], gain[:, :].unsqueeze(1).to_broadcast([P, UNITS, NE]), ALU.mult))
            link(v.tensor_reduce(pk_sum[:, :], past[:, :, :], AX.X, ALU.add))
            link(v.scalar_tensor_tensor(out=pk_i[:, :], in0=unit_no[:, :], scalar=float(P), in1=pk_sum[:, :], op0=ALU.mult, op1=ALU.add))
            inc(v.tensor_scalar(unit_row[:, :], pk_i[:, :], (1 << SHIFT) - 1, None, ALU.bitwise_and))
            link(v.tensor_scalar(unit_w[:, :], pk_i[:, :], SHIFT, None, ALU.arith_shift_right))
            inc(v.tensor_copy(unit_ef[:, :], unit_w[:, :]))
            v.tensor_scalar(unit_e[:, :], unit_w[:, :], float(NE - 1), None, ALU.min).then_inc(table_ready, 1)
            wait()

            N0 = TOK // P

            def x_copy(j, i, first):
                n_ = j * QU + i
                dv.wait_ge(xbT_ps, n_ + 1)
                v.tensor_copy(xbT[:, i % 2, :], bank_t[i % 2][:, 0:E]).then_inc(xbT_sb, 1)
                if not first:
                    dv.wait_ge(y_out[i], j * 16)
                c = inc(v.tensor_scalar(other[i][:, :], xb[i][:, E + 1:E + 2], unit_ef[:, ds(n_, 1)], None, ALU.not_equal))
                v.tensor_scalar(yi[i][:, :], xb[i][:, E + 1:E + 2], unit_ef[:, ds(n_, 1)], xb[i][:, E:E + 1], ALU.not_equal, ALU.add)
                wait(c)
                v.tensor_scalar(yw[i][:, :], other[i][:, :], xb[i][:, E + 3:E + 4], xb[i][:, E + 2:E + 3], ALU.mult, ALU.add).then_inc(yi_sb, 1)

            dv.wait_ge(xb_in[0], 16)
            x_copy(0, 0, True)
            for i in range(1, QU):
                x_copy(0, i, True)
                hidden(N0 + i - 1, (i - 1) % 2)
            start = base[0] + n[0]
            with dv.Fori(1, UNITS // QU) as j:
                base[0], n[0] = (j - 1) * QU + start, 0
                for i in range(QU):
                    x_copy(j, i, False)
                    hidden(j * QU + (i + N0 - 1), (i - 1) % 2)
                assert n[0] == QU
            base[0], n[0] = start + (UNITS // QU - 1) * QU, 0
            hidden(UNITS - 1 + N0, (UNITS - 1) % 2)

            def combine(b, i, first):
                def y(t):
                    return cbuf[i + t // NT][:, (NT + t % NT) * E:(NT + t % NT + 1) * E]

                def strand():
                    for h in range(2):
                        dv.wait_ge(y1_in[i + h], (b - i) * 4 + 16)
                    yield from stats(y, st_c, mv_c, ve[:, :], 2 * NT)
                    yield from rsqrt(r_c[:, :], ve[:, :], nt_[:, :])

                for _ in strand():
                    pass
                link(v.tensor_tensor(ve[:, :], mv_c[:, :, 0], r_c[:, :], ALU.mult))
                if not first:
                    dv.wait_ge(out_add, of(b, NT))
                for h in range(2):
                    v.tensor_tensor(shift[:, h * NT:(h + 1) * NT], cbuf[i + h][:, 2 * NT * E:2 * NT * E + NT], ve[:, h * NT:(h + 1) * NT], ALU.subtract)
                for t in range(2 * NT):
                    if t % NT == 0 and is_int(b) is False:
                        dv.wait_ge(stored[i + t // NT], (b - i) * 4)
                    v.scalar_tensor_tensor(out=res[i + t // NT][:, t % NT, :], in0=y(t), scalar=r_c[:, t:t + 1], in1=cbuf[i + t // NT][:, (t % NT) * E:(t % NT + 1) * E],
                                           op0=ALU.mult, op1=ALU.add).then_inc(res_ready, 1)

            combine(0, 0, True)
            combine(2, 2, False)
            start = base[0] + n[0]
            with dv.Fori(1, B // 4) as j:
                base[0], n[0] = (j - 1) * DVE_C + start, 0
                combine(j * 4, 0, False)
                combine(j * 4 + 2, 2, False)
                assert n[0] == DVE_C, f"DVE_C = {n[0]}"


_INS = ['L0_attn_x', 'L0_attn_W_qkv', 'L0_attn_b_qkv', 'L0_attn_W_proj', 'L0_attn_b_proj', 'L0_ffn_ln_scale',
        'L0_ffn_ln_bias', 'L0_ffn_gate_w', 'L0_ffn_Wg', 'L0_ffn_Wu', 'L0_ffn_Wd', 'L0_ffn_sWg', 'L0_ffn_sWu', 'L0_ffn_sWd']


def kernel(**inputs):
    import numpy as _np
    import concourse.bacc as _bacc
    from concourse import mybir as _mybir
    from concourse.bass_utils import run_bass_kernel_spmd as _run

    nc = _bacc.Bacc("TRN2", target_bir_lowering=False, num_devices=1)
    arrays, args = {}, []
    for name in _INS:
        a = _np.ascontiguousarray(inputs[name])
        arrays[f"in_{name}"] = a
        args.append(nc.dram_tensor(f"in_{name}", a.shape, _mybir.dt.from_np(a.dtype), kind="ExternalInput").ap())
    args.append(nc.dram_tensor("out_dram", (B, S, E), _mybir.dt.float32, kind="ExternalOutput").ap())
    program(nc, *args)
    r = _run(nc, [arrays], core_ids=[0])
    return r.results[0]["out_dram"]
```

```python
import concourse.bass as bass
from concourse import mybir
from contextlib import ExitStack

P = 128
E = 128
B, S = 8, 1024
NT = S // P
HEADS, D = 16, 8
INTER = 256
IC = INTER // P
NE = 8
TOK = B * S
CAP = TOK + P
ROW = E + 4
UNITS = 2 * TOK // P + NE
SLOTS = NE * CAP + NE * P
PADS = 2 * (NE * P + NE * P)
C_AHEAD = 3
C_ADD_AT = (1, 5)
POOL_ADDS = 6
C_GROUPS = ((0, 2, 8), (2, 2, 8), (4, 2, 8), (6, 1, 5), (7, 1, 5))
QU = 8
GROUPS = UNITS // QU
HALF = QU // 2
LN_EPS = 1e-5
EPS = 1e-5
SHIFT = 17
PHI_AT = (17, 21, 24, 27, 31, 35, 39)
WEIGHTS_AT = (20, 26, 28, 30, 32, 34, 37)
ROUTER_AT = (40, 47, 48, 49, 50, 51, 52, 53, 54, 55, 56, 57, 58, 59, 60, 64, 65, 66, 67, 68, 69, 70, 72, 73, 74, 75, 76, 77, 78, 79, 80)
PRODUCTS_AT = (54, 60, 66, 72, 78, 84, 90, 96, 102)
SLOTS_AT = (93, 94, 95, 96)
XN_DVE = 4
RANK_AT = 5
SETUP_AT = (21, 22, 23, 24, 25, 26, 27, 28, 29, 30, 31, 32)
LATE = 2
LATE_EARLY = 3
LATE_EARLY_AT = (10, 18, 26)
COUNT_AT = 4
TABLE_AT = 2
PACK_AT = 5
XNT_AT = 8
Q_AT = 9
XN_AT = 7
DVE_PAIR = 232
KEEP = 2 * NT * E + NT


def program(nc, x, w_qkv, b_qkv, w_proj, b_proj, ln_scale, ln_bias, gate_w, wg, wu, wd, swg, swu, swd, out):
    f32, f32r, bf16, i32 = mybir.dt.float32, mybir.dt.float32r, mybir.dt.bfloat16, mybir.dt.int32
    ALU, ACT, AX = mybir.AluOpType, mybir.ActivationFunctionType, mybir.AxisListType
    ds = bass.ds

    x_v = x.rearrange("b (p t) f -> b p (t f)", t=NT)
    out_v = out.rearrange("b (p t) f -> b p (t f)", t=NT)
    slots_dram = nc.dram_tensor("slots_dram", (SLOTS, ROW), f32, kind="Internal").ap()
    routed_dram = nc.dram_tensor("routed_dram", (2 * TOK + PADS, E), f32, kind="Internal").ap()
    routed_v = routed_dram[0:2 * TOK, :].rearrange("(b p t) f -> b p (t f)", b=B, p=P)

    ctx = ExitStack()
    with ctx:
        def sb(name, shape, dt=f32):
            return ctx.enter_context(nc.sbuf_tensor(name, shape, dt))

        def pb(name):
            return ctx.enter_context(nc.psum_tensor(name, [P, 512], f32))

        def sem(name):
            return ctx.enter_context(nc.semaphore(name))

        wqkv = sb("wqkv", [P, 3 * E])
        wgu = [sb("wgu_hi", [P, NE, 2 * INTER], f32r), sb("wgu_lo", [P, NE, 2 * INTER], f32r)]
        wdn = sb("wdn", [P, NE, IC * E])
        swgu = sb("swgu", [P, 2 * INTER])
        swdn = sb("swdn", [P, IC * E])
        ident = sb("ident", [P, P])
        ones = sb("ones", [P, P])
        ones_bf = sb("ones_bf", [P, 512], bf16)
        tri = sb("tri", [P, P], bf16)
        head_mask = sb("head_mask", [P, HEADS])
        bias3 = sb("bias3", [P, 3 * E])
        bias_bf = sb("bias_bf", [P, 3 * E], bf16)
        bias_part = sb("bias_part", [P, 3 * E], bf16)
        bias_acc = sb("bias_acc", [P, 3 * E])
        gate_t = sb("gate_t", [P, NE])
        gate_s = sb("gate_s", [P, NE])
        gate_c = sb("gate_c", [P, NE])
        gate_b = sb("gate_b", [P, NE])
        ln_sc = sb("ln_sc", [P, 1])
        ln_bi = sb("ln_bi", [P, 1])
        ln_bi_w = sb("ln_bi_w", [P, P])
        minus1 = sb("minus1", [P, 1])
        rank_of = sb("rank_of", [P, NE])
        region = sb("region", [P, NE])
        tok2 = sb("tok2", [P, B * NT])
        powers = sb("powers", [P, QU])
        lower8 = sb("lower8", [P, NE, NE])
        unit_no = sb("unit_no", [P, UNITS])
        pad_rows = sb("pad_rows", [P, NE, ROW])

        keep = sb("keep", [P, B, KEEP])
        gu_stage = keep[:, B - 2:B, 0:NE // 2 * 2 * INTER]
        xin = [sb(f"xin{i}", [P, NT, E]) for i in range(2)]
        u_row = [sb(f"u_row{i}", [P, NT, ROW]) for i in range(2)]
        slot_i = [sb(f"slot_i{i}", [P, 2 * NT], i32) for i in range(2)]
        spare_rows = u_row[1]
        xn = sb("xn", [P, NT, E])
        xnT = sb("xnT", [P, S])
        q_e = sb("q_e", [P, 2, 512])
        k_e = sb("k_e", [P, 2, 2, E])
        pqT = sb("pqT", [P, S])
        pk = sb("pk", [P, NT, E])
        v1 = sb("v1", [P, NT, E + 1])
        kvm = sb("kvm", [P, E + HEADS])
        att = sb("att", [P, NT, E])
        zt = sb("zt", [P, 2, 2, HEADS])
        zr = sb("zr", [P, 2, 2, HEADS])
        nb_u = sb("nb_u", [P, NT])
        nb_x = sb("nb_x", [P, NT])
        uT = sb("uT", [P, S])
        st_a = sb("st_a", [P, NT, 6])
        st_1 = sb("st_1", [P, NT, 6])
        mv_a = sb("mv_a", [P, NT, 2])
        mv_u = sb("mv_u", [P, NT, 2])
        mv_1 = sb("mv_1", [P, NT, 2])
        ve = sb("ve", [P, 2 * NT])
        rs = sb("rs", [P, 2 * NT])
        nt_ = sb("nt_", [P, 2 * NT])
        r_u = sb("r_u", [P, NT])
        r_ax = sb("r_ax", [P, 2 * NT])
        r_4 = sb("r_4", [P, NT])
        ve_u = sb("ve_u", [P, NT])
        ve_4 = sb("ve_4", [P, NT])
        nt_u = sb("nt_u", [P, NT])
        nt_4 = sb("nt_4", [P, NT])
        lg = sb("lg", [P, NT, NE])
        lg2 = sb("lg2", [P, NT, NE])
        cand = sb("cand", [P, NT, NE])
        oh1 = sb("oh1", [P, NT, NE])
        oh2 = sb("oh2", [P, NT, NE])
        oh_bf = sb("oh_bf", [P, NT, NE], bf16)
        total = sb("total", [P, NE])
        total_new = sb("total_new", [P, NE])
        total_bf = sb("total_bf", [P, NE], bf16)
        m1 = sb("m1", [P, NT])
        m2 = sb("m2", [P, NT])
        i1 = sb("i1", [P, NT])
        i2 = sb("i2", [P, NT])
        r_in = sb("r_in", [P, NT, NE + 1])
        r_exp = sb("r_exp", [P, NT, NE + 1])
        esum = sb("esum", [P, NT])
        den = sb("den", [P, NT])
        wden = sb("wden", [P, NT])
        pos = sb("pos", [P, NT, NE])
        slot_f = sb("slot_f", [P, 2 * NT])
        act_g = sb("act_g", [P, 2, INTER])
        hid = sb("hid", [P, 2, INTER])
        hidT = sb("hidT", [P, 2, INTER])
        xb = u_row[0]
        yb = att
        xbT = [sb("xbT_hi", [P, 2, P], f32r), sb("xbT_lo", [P, 2, P], f32r)]
        yi = sb("yi", [P, QU], i32)
        other = sb("other", [P, QU])
        yw = sb("yw", [P, QU])
        cnt = sb("cnt", [P, NE])
        tl_i = sb("tl_i", [P, NE], i32)
        tl_s = sb("tl_s", [P, NE], i32)
        tl = sb("tl", [P, NE])
        tl8 = sb("tl8", [P, NE, NE])
        cum = sb("cum", [P, NE])
        gain = sb("gain", [P, NE])
        past = sb("past", [P, UNITS, NE])
        pk_sum = sb("pk_sum", [P, UNITS])
        pk_i = sb("pk_i", [P, UNITS], i32)
        unit_row = sb("unit_row", [P, UNITS], i32)
        unit_e = sb("unit_e", [P, 2 + UNITS])
        own_terms = sb("own_terms", [P, GROUPS, QU])
        own_f = sb("own_f", [P, GROUPS])
        own_i = sb("own_i", [P, GROUPS], i32)
        before_i = sb("before_i", [P, GROUPS], i32)
        unit_pack = sb("unit_pack", [P, GROUPS], i32)
        unit_ef = sb("unit_ef", [P, UNITS])
        unit_w = sb("unit_w", [P, UNITS], i32)
        pad_f = sb("pad_f", [P, NE])
        pad_i = sb("pad_i", [P, NE], i32)
        shift = sb("shift", [P, 2, 2 * NT])
        st_c = sb("st_c", [P, 2 * NT, 6])
        mv_c = sb("mv_c", [P, 2 * NT, 2])
        r_c = sb("r_c", [P, 2, 2 * NT])

        bank_t = [pb("bank_t0"), pb("bank_t1")]
        bank_p = [pb("bank_p0"), pb("bank_p1")]
        bank_g = [pb("bank_g0"), pb("bank_g1")]
        bank_h = [pb("bank_h0"), pb("bank_h1")]

        w_loaded, sw_loaded, ew_loaded = sem("w_loaded"), sem("sw_loaded"), sem("ew_loaded")
        x_loaded = [sem("x_loaded0"), sem("x_loaded1")]
        consts = sem("consts")
        spare_in = sem("spare_in")
        setup = sem("setup")
        setup_ps = sem("setup_ps")
        attn_ps, xnT_ps, q_ps, kv_ps, sum_ps = sem("attn_ps"), sem("xnT_ps"), sem("q_ps"), sem("kv_ps"), sem("sum_ps")
        uT_ps, logit_ps, rank_ps = sem("uT_ps"), sem("logit_ps"), sem("rank_ps")
        gu_ps, ht_ps, y_ps, xbT_ps = sem("gu_ps"), sem("ht_ps"), sem("y_ps"), sem("xbT_ps")
        cnt_ps = sem("cnt_ps")
        xnT_sb, q_exp, kv_exp, uT_sb, r_done = sem("xnT_sb"), sem("q_exp"), sem("kv_exp"), sem("uT_sb"), sem("r_done")
        xbT_hi = sem("xbT_hi")
        silu, ht_sb, y_sb = sem("silu"), sem("ht_sb"), sem("y_sb")
        y_normed = sem("y_normed")
        pool_added = sem("pool_added")
        u_norm, x_norm = sem("u_norm"), sem("x_norm")
        u_dve, u_act, xn_dve, xn_act = sem("u_dve"), sem("u_act"), sem("xn_dve"), sem("xn_act")
        logit_read, rank_read = sem("logit_read"), sem("rank_read")
        dve = sem("dve")
        sp_passed = sem("sp_passed")
        dve_passed, pool_passed = sem("dve_passed"), sem("pool_passed")
        att_sb, pq_sb, pk_sb, kvm_sb = sem("att_sb"), sem("pq_sb"), sem("pk_sb"), sem("kvm_sb")
        x1_done = sem("x1_done")
        r_ready, oh_ready, slots_ready, rc_ready = sem("r_ready"), sem("oh_ready"), sem("slots_ready"), sem("rc_ready")
        hid_sb, xbT_lo, yi_sb = sem("hid_sb"), sem("xbT_lo"), sem("yi_sb")
        w_split = sem("w_split")
        pads_ready, table_ready = sem("pads_ready"), sem("table_ready")
        res_ready = sem("res_ready")
        scattered = [sem("scattered0"), sem("scattered1")]
        pads_in = sem("pads_in")
        xb_in = [sem("xb_in0"), sem("xb_in1")]
        y_out = [sem("y_out0"), sem("y_out1")]
        stored = sem("stored")
        y0_in, y1_in = [sem(f"y0_in{b}") for b in range(B)], [sem(f"y1_in{b}") for b in range(B)]

        def of(b, n, k=0):
            return b * n + k

        def is_int(b):
            return isinstance(b, int)

        def late(b):
            return is_int(b) and b >= B - LATE

        def uT_at(b):
            return xnT if is_int(b) and b == B - 1 else uT

        def kept(b, a, z):
            return keep[:, ds(b, 1), a:z].rearrange("p b n -> p (b n)")

        def schedule(eng, step):
            for s in range(3):
                step(s, s % 2)
            with eng.Fori(0, (B - 4) // 2) as j:
                step(j * 2 + 3, 1)
                step(j * 2 + 4, 0)
            for s in range(B - 1, B + 2):
                step(s, s % 2)

        def has(b):
            return not is_int(b) or 0 <= b < B

        block = ctx.enter_context(nc.Block())

        @block.sync
        def _(sp):
            sp.dma_start(xin[0][:, :, :], x_v[0, :, :]).then_inc(x_loaded[0], 16)
            sp.dma_start(wqkv[:, :], w_qkv).then_inc(w_loaded, 16)
            for i in range(3):
                sp.dma_start(bias3[i:i + 1, :], b_qkv.rearrange("(a n) -> a n", a=1)).then_inc(w_loaded, 16)
            sp.dma_start(gate_t[:, :], gate_w.rearrange("e f -> f e"), allow_slow_non_contiguous=True).then_inc(w_loaded, 16)
            sp.dma_start(ln_sc[:, :], ln_scale.rearrange("(f a) -> f a", a=1)).then_inc(w_loaded, 16)
            sp.dma_start(ln_bi[:, :], ln_bias.rearrange("(f a) -> f a", a=1)).then_inc(w_loaded, 16)
            sp.dma_start(xin[1][:, :, :], x_v[1, :, :]).then_inc(x_loaded[1], 16)
            sp.dma_start(swgu[:, 0:INTER], swg).then_inc(sw_loaded, 16)
            sp.dma_start(swgu[:, INTER:2 * INTER], swu).then_inc(sw_loaded, 16)
            sp.dma_start(swdn[:, :].rearrange("p (c n) -> p c n", c=IC), swd.rearrange("(c p) n -> p c n", p=P)).then_inc(sw_loaded, 16)
            for h in range(2):
                e = slice(h * NE // 2, (h + 1) * NE // 2)
                stage = gu_stage[:, h, :].rearrange("p (e n) -> p e n", e=NE // 2)
                sp.dma_start(stage[:, :, 0:INTER], wg[e, :, :].rearrange("e p n -> p e n")).then_inc(ew_loaded, 16)
                sp.dma_start(stage[:, :, INTER:2 * INTER], wu[e, :, :].rearrange("e p n -> p e n")).then_inc(ew_loaded, 16)
            for e in range(NE):
                sp.dma_start(wdn[:, e, :].rearrange("p (c n) -> p c n", c=IC), wd[e, :, :].rearrange("(c p) n -> p c n", p=P)).then_inc(ew_loaded, 16)
            sp.wait_ge(consts, 1)
            sp.dma_start(slots_dram[NE * CAP:SLOTS, :].rearrange("(p e) n -> p (e n)", p=P),
                         spare_rows[:, :, :].rearrange("p e n -> p (e n)")).then_inc(spare_in, 16)

            def step(s, par):
                if has(s - 1) and has(s) and has(s + 1):
                    sp.wait_ge(x1_done, s)
                    sp.dma_start(xin[1 - par][:, :, :], x_v[ds(s + 1, 1), :, :].rearrange("b p (t n) -> (b p) t n", t=NT)).then_inc(x_loaded[1 - par], 16)

            schedule(sp, step)

            sp.wait_ge(pads_ready, 1)
            for e in range(NE):
                row = sp.value_load(pad_i[0:1, e:e + 1], min_val=0, max_val=NE * CAP - P)
                sp.dma_start(slots_dram[ds(row, P), :], pad_rows[:, e, :]).then_inc(pads_in, 16)

            sp.wait_ge(table_ready, 1)
            sp.wait_ge(pads_in, 16 * NE)
            sp.wait_ge(spare_in, 16)
            for i in range(2):
                sp.wait_ge(scattered[i], 16 * 2 * NT * (B // 2))

            def load_unit(n, i):
                row = sp.value_load(unit_row[0:1, ds(n, 1)], min_val=0, max_val=SLOTS - P)
                sp.dma_start(xb[:, i, :], slots_dram[ds(row, P), :]).then_inc(xb_in[i // HALF], 16)

            for i in range(QU):
                load_unit(i, i)
            with sp.Fori(1, GROUPS) as j:
                for i in range(QU):
                    if i % HALF == 0:
                        sp.wait_ge(yi_sb, of(j, 2, i // HALF - 1))
                        sp.sem_inc(sp_passed, 1)
                    sp.wait_ge(xbT_ps, of(j, QU, i - QU + 1))
                    load_unit(j * QU + i, i)

            for b in range(B):
                if b < POOL_ADDS:
                    sp.wait_ge(pool_added, b + 1)
                else:
                    sp.wait_ge(res_ready, b - POOL_ADDS + 1)
                sp.dma_start(out_v[b, :, :], kept(b, 0, NT * E)).then_inc(stored, 16)
            sp.wait_ge(stored, 16 * B)

        @block.gpsimd
        def _(pool):
            g = nc.gpsimd
            n = [0]

            def link(ins):
                n[0] += 1
                ins.then_inc(setup, 1)

            link(g.memset(ident[:, :], 0.0))
            link(g.memset(ones[:, :], 1.0))
            link(g.memset(ones_bf[:, :], 1.0))
            link(g.memset(tri[:, :], 1.0))
            link(g.memset(head_mask[:, :], 1.0))
            link(g.memset(lower8[:, :, :], 1.0))
            link(g.memset(spare_rows[:, :, :], 0.0))
            link(g.memset(pad_rows[:, :, :], 0.0))
            link(g.memset(v1[:, :, E:E + 1], 1.0))
            link(g.memset(total[:, :], 0.0))
            link(g.memset(total_bf[:, :], 0.0))
            link(g.iota(rank_of[:, :], [[-1, NE]], base=NE, channel_multiplier=0, allow_small_or_imprecise_dtypes=True))
            for e in range(NE):
                link(g.memset(region[:, e:e + 1], float(e * CAP)))
            for i in range(QU):
                link(g.memset(powers[:, i:i + 1], float(NE ** i)))
            link(g.memset(unit_e[:, 0:2], 0.0))
            link(g.iota(tok2[:, :].rearrange("p (b t) -> p b t", b=B), [[2 * S, B], [2, NT]], base=0, channel_multiplier=2 * NT, allow_small_or_imprecise_dtypes=True))
            link(g.iota(unit_no[:, :], [[1, UNITS]], base=0, channel_multiplier=0, allow_small_or_imprecise_dtypes=True))
            pool.wait_ge(setup, n[0])
            link(g.affine_select(out=ident[:, :], in_=ident[:, :], compare_op=ALU.not_equal, fill=1.0, base=0, pattern=[[-1, P]], channel_multiplier=1))
            link(g.affine_select(out=tri[:, :], in_=tri[:, :], compare_op=ALU.is_gt, fill=0.0, base=0, pattern=[[1, P]], channel_multiplier=-1))
            link(g.affine_select(out=lower8[:, :, :], in_=lower8[:, :, :], compare_op=ALU.is_ge, fill=0.0, base=0, pattern=[[1, NE], [-1, NE]], channel_multiplier=0))
            link(g.affine_select(out=head_mask[:, :], in_=head_mask[:, :], compare_op=ALU.is_ge, fill=0.0, base=0, pattern=[[-D, HEADS]], channel_multiplier=1))
            link(g.iota(pad_rows[:, :, E:E + 1], [[2 * P, NE], [0, 1]], base=2 * TOK, channel_multiplier=2, allow_small_or_imprecise_dtypes=True))
            link(g.iota(spare_rows[:, :, E:E + 1], [[2, NE], [0, 1]], base=2 * TOK + 2 * NE * P, channel_multiplier=2 * NE, allow_small_or_imprecise_dtypes=True))
            pool.wait_ge(setup, n[0])
            g.affine_select(out=head_mask[:, :], in_=head_mask[:, :], compare_op=ALU.is_ge, fill=0.0, base=D - 1, pattern=[[D, HEADS]], channel_multiplier=-1).then_inc(consts, 1)

            pool.wait_ge(ew_loaded, 16 * (4 + NE))
            halves = [(gu_stage[:, h, :], [w[:, h * NE // 2:(h + 1) * NE // 2, :].rearrange("p e n -> p (e n)") for w in wgu]) for h in range(2)]
            for stage, (hi, _) in halves:
                g.tensor_copy(hi, stage).then_inc(w_split, 1)
            pool.wait_ge(w_split, 2)
            for stage, (hi, lo) in halves:
                g.tensor_tensor(lo, stage, hi.bitcast(f32), ALU.subtract).then_inc(w_split, 1)

            def scatter(k, par):
                pool.wait_ge(slots_ready, of(k, 1, 1))
                pool.sem_inc(pool_passed, 1)
                for t in range(NT):
                    for c in range(2):
                        g.indirect_dma_start(slots_dram, bass.IndirectOffsetOnAxis(ap=slot_i[par][:, c * NT + t:c * NT + t + 1], axis=0),
                                             u_row[par][:, t, :], None).then_inc(scattered[par], 16)

            with pool.Fori(0, B // 2) as j:
                scatter(j * 2, 0)
                scatter(j * 2 + 1, 1)

            def scatter_y(n_, i, half):
                pool.wait_ge(y_sb, n_ + TOK // P + 1)
                pool.wait_ge(yi_sb, half)
                pool.sem_inc(pool_passed, 1)
                g.indirect_dma_start(routed_dram, bass.IndirectOffsetOnAxis(ap=yi[:, i:i + 1], axis=0), yb[:, i, :], None).then_inc(y_out[i // HALF], 16)

            with pool.Fori(0, GROUPS) as j:
                for i in range(QU):
                    scatter_y(j * QU + i, i, j * 2 + (i // HALF + 1))

            for i in range(2):
                pool.wait_ge(y_out[i], 16 * HALF * (GROUPS))

            def add_rows(b, c, in_):
                pool.dma_start(kept(b, NT * E, 2 * NT * E).rearrange("p (t n) -> p t n", n=E), routed_v[b, :, :].rearrange("p (t c n) -> p t c n", c=2, n=E)[:, :, c, :],
                               accum_op=ALU.add).then_inc(in_[b], 16)

            for b in range(C_AHEAD):
                add_rows(b, 0, y0_in)
            for b in range(B):
                pool.wait_ge(y0_in[b], 16)
                add_rows(b, 1, y1_in)
                if b + C_AHEAD < B:
                    add_rows(b + C_AHEAD, 0, y0_in)
            for b in range(POOL_ADDS):
                pool.wait_ge(y_normed, b + 1)
                g.tensor_tensor(kept(b, 0, NT * E), kept(b, 0, NT * E), kept(b, NT * E, 2 * NT * E), ALU.add).then_inc(pool_added, 1)

        @block.tensor
        def _(pe):
            mm = nc.tensor.matmul
            pe.wait_ge(consts, 1)
            pe.wait_ge(setup_ps, 1)
            mm(bank_h[0][:, 0:NE], ones[:, :], gate_s[:, :], start=True, stop=True)
            mm(bank_h[0][:, NE:2 * NE], ln_bi_w[:, :], gate_t[:, :], start=True, stop=True).then_inc(setup_ps, 1)

            def attn(k, uses):
                pe.wait_ge(kvm_sb, of(k, 1, 1))
                pe.wait_ge(pq_sb, of(k, 2, 2))
                for i in uses:
                    if i < 2:
                        pe.wait_ge(pk_sb, of(k, 4, 4))
                    else:
                        pe.wait_ge(att_sb, of(k, 4, i - 1))
                    for h in range(2):
                        t = 2 * i + h
                        last = mm(bank_p[i % 2][:, 256 * h:256 * h + E + HEADS], pqT[:, t * P:(t + 1) * P], kvm[:, :], start=True, stop=True)
                    last.then_inc(attn_ps, 1)

            def transpose_xn(f):
                pe.wait_ge(xn_dve, of(f, 1, 1))
                pe.wait_ge(xn_act, of(f, 1, 1))
                for i in range(2):
                    if has(f - 2):
                        if i == 0:
                            pe.wait_ge(uT_sb, of(f, 2, -2))
                        else:
                            pe.wait_ge(rank_read, f - 1)
                    elif has(f - 1):
                        if i == 0:
                            pe.wait_ge(kvm_sb, f)
                        else:
                            pe.wait_ge(xnT_sb, 2 * f)
                    for t in range(4 * i, 4 * i + 4):
                        last = nc.tensor.transpose(bank_t[i][:, (t % 4) * P:(t % 4 + 1) * P], xn[:, t, :], ident[:, :])
                    last.then_inc(xnT_ps, 1)

            def queries(f):
                for i in range(2):
                    pe.wait_ge(xnT_sb, of(f, 2, i + 1))
                    if not is_int(f) or f > 0:
                        pe.wait_ge(att_sb, of(f, 4, i - 1))
                    mm(bank_p[i][:, :], bias_bf[:, 0:E], ones_bf[:, :], start=True, stop=False)
                    mm(bank_p[i][:, :], wqkv[:, 0:E], xnT[:, i * 512:(i + 1) * 512], start=False, stop=True).then_inc(q_ps, 1)

            def keys_values(f):
                for i in range(4):
                    if i < 2:
                        pe.wait_ge(pq_sb, of(f, 2, i + 1))
                    else:
                        pe.wait_ge(pk_sb, of(f, 4, i - 1))
                    for h in range(2):
                        t = 2 * i + h
                        o = bank_p[i % 2][:, 256 * h:256 * h + 256]
                        mm(o, ones_bf[:, 0:P], bias_bf[:, E:3 * E], start=True, stop=False)
                        last = mm(o, xnT[:, t * P:(t + 1) * P], wqkv[:, E:3 * E], start=False, stop=True)
                    last.then_inc(kv_ps, 1)
                for t in range(NT):
                    if t % 2 == 0:
                        pe.wait_ge(pk_sb, of(f, 4, t // 2 + 1))
                    last = mm(bank_t[0][:, 0:E + 1], pk[:, t, :], v1[:, t, :], start=t == 0, stop=t == NT - 1)
                last.then_inc(sum_ps, 1)

            def gate_up(n_, i, xT, w):
                if not is_int(n_) or n_ >= 2:
                    pe.wait_ge(hid_sb, n_ - 1)
                mm(bank_g[i][:, :], xT, w, start=True, stop=True).then_inc(gu_ps, 1)

            def hid_t(n_, i, ordered=False):
                pe.wait_ge(hid_sb, n_ + 1)
                if not ordered and (not is_int(n_) or n_ >= 2):
                    pe.wait_ge(ht_sb, n_ - 1)
                for c in range(IC):
                    last = nc.tensor.transpose(bank_h[i][:, c * P:(c + 1) * P], hid[:, i, c * P:(c + 1) * P], ident[:, :])
                last.then_inc(ht_ps, 1)

            def down(n_, i, w, ordered=False):
                pe.wait_ge(ht_sb, n_ + 1)
                if not ordered and (not is_int(n_) or n_ >= 2):
                    pe.wait_ge(y_sb, n_ - 1)
                for c in range(IC):
                    last = mm(bank_h[i][:, INTER:INTER + E], hidT[:, i, c * P:(c + 1) * P], w(c), start=c == 0, stop=c == IC - 1)
                last.then_inc(y_ps, 1)

            def transpose_u(k, par, uses):
                for i in uses:
                    pe.wait_ge(u_act if i else u_dve, of(k, 1, 1))
                    if i == 1 and has(k + 1):
                        pe.wait_ge(kvm_sb, of(k, 1, 2))
                    for t in range(4 * i, 4 * i + 4):
                        last = nc.tensor.transpose(bank_t[1 - i][:, (t % 4) * P:(t % 4 + 1) * P], u_row[par][:, t, 0:E], ident[:, :])
                    last.then_inc(uT_ps, 1)

            def logits(k):
                pe.wait_ge(uT_sb, of(k, 2, 2))
                for t in range(NT):
                    last = mm(bank_t[1][:, t * NE:(t + 1) * NE], uT_at(k)[:, t * P:(t + 1) * P], gate_c[:, :], start=True, stop=True)
                last.then_inc(logit_ps, 1)

            def ranks(m):
                pe.wait_ge(oh_ready, of(m, 1, 1))
                o = bank_t[1]
                oh = oh_bf[:, :, :].rearrange("p t e -> p (t e)")
                mm(o[:, 64:128], tri[:, :], oh, start=True, stop=False)
                for s in range(1, NT):
                    mm(o[:, 64 + s * NE:128], ones_bf[:, 0:P], oh[:, 0:(NT - s) * NE], start=False, stop=False)
                mm(o[:, 64:128], ones_bf[:, 0:P], total_bf[:, :].unsqueeze(1).to_broadcast([P, NT, NE]), start=False, stop=True).then_inc(rank_ps, 1)

            def step(s, par):
                m = s - 1
                if has(s):
                    keys_values(s)
                if is_int(s) and s == B:
                    late_units(0, LATE_EARLY)
                if has(m):
                    transpose_u(m, 1 - par, range(1))
                if has(s):
                    attn(s, range(2))
                own = has(m) and not late(m)
                for t in range(NT + 2):
                    n_ = m * NT + t
                    if own and t < NT:
                        if t == 0:
                            pe.wait_ge(uT_sb, of(m, 2, 1))
                        gate_up(n_, t % 2, uT[:, t * P:(t + 1) * P], swgu[:, :])
                    if t < 2 and has(s):
                        attn(s, range(t + 2, t + 3))
                    if t == 1 and has(m):
                        transpose_u(m, 1 - par, range(1, 2))
                        logits(m)
                    if own and t >= 2:
                        down(n_ - 2, t % 2, lambda c: swdn[:, c * E:(c + 1) * E])
                    if own and 1 <= t <= NT:
                        hid_t(n_ - 1, (t - 1) % 2)
                    if has(m) and t == RANK_AT:
                        ranks(m)
                    if has(s + 1) and t == XNT_AT:
                        transpose_xn(s + 1)
                    if has(s + 1) and t == Q_AT:
                        queries(s + 1)

            def late_units(a, z):
                for i in range(a, z):
                    n_ = (B - LATE) * NT + i
                    if i < LATE * NT:
                        gate_up(n_, i % 2, uT_at(n_ // NT)[:, i % NT * P:(i % NT + 1) * P], swgu[:, :])
                    if i >= 2:
                        down(n_ - 2, i % 2, lambda c: swdn[:, c * E:(c + 1) * E])
                    if 1 <= i <= LATE * NT:
                        hid_t(n_ - 1, (i - 1) % 2)
                    if i == COUNT_AT:
                        pe.wait_ge(oh_ready, B + 1)
                        mm(bank_t[0][:, 0:NE], ones_bf[:, 0:P], total_bf[:, :], start=True, stop=True).then_inc(cnt_ps, 1)

            pe.wait_ge(setup_ps, 3)
            pe.wait_ge(w_loaded, 16 * 7)
            pe.wait_ge(sw_loaded, 16 * 3)
            transpose_xn(0)
            queries(0)
            schedule(pe, step)

            late_units(LATE_EARLY, LATE * NT + 2)

            N0 = TOK // P
            pe.wait_ge(w_split, 4)
            pe.wait_ge(table_ready, 1)

            pack_reg = pe.alloc_register("pack")

            def load_pack(j):
                pe.reg_load(pack_reg, unit_pack[0:1, ds(j, 1)])

            def group_experts():
                at = {i: 3 * (i if i >= 0 else QU + 2 + i) for i in range(-2, QU)}
                number = pe.snap(pack_reg, min_val=0, max_val=(1 << 3 * (QU + 2)) - 1)
                return {i: ((number >> at[i]) & (NE - 1)).with_bounds(min_val=0, max_val=NE - 1) for i in at}

            def transpose_x(j, i):
                if i % HALF == 0:
                    pe.wait_ge(xb_in[i % QU // HALF], (j + i // QU) * 16 * HALF + 16 * HALF)
                nc.tensor.transpose(bank_t[i % 2][:, 0:E], xb[:, i % QU, 0:E], ident[:, :]).then_inc(xbT_ps, 1)

            def routed_down(n_, i, e):
                down(n_ + N0, i, lambda c: wdn[:, ds(e, 1), c * E:(c + 1) * E].rearrange("p e n -> p (e n)"), ordered=True)

            def group(j, first, final):
                e = group_experts()
                for i in range(QU):
                    n_ = j * QU + i
                    if not (final and i == QU - 1):
                        transpose_x(j, i + 1)
                    pe.wait_ge(xbT_lo, n_ + N0)
                    for a, b_ in ((1, 0), (0, 0), (0, 1)):
                        last = mm(bank_g[i % 2][:, :], xbT[a][:, i % 2, :], wgu[b_][:, ds(e[i], 1), :].rearrange("p e n -> p (e n)"), start=a == 1, stop=b_ == 1)
                    last.then_inc(gu_ps, 1)
                    if i == PACK_AT and not final:
                        load_pack(j + 1)
                    if not first or i >= 2:
                        routed_down(n_ - 2, i % 2, e[i - 2])
                    if not first or i >= 1:
                        hid_t(n_ + N0 - 1, (i + 1) % 2, ordered=True)
                return e

            load_pack(0)
            transpose_x(0, 0)
            NJ = GROUPS
            group(0, True, False)
            with pe.Fori(1, NJ - 1) as j:
                group(j, False, False)
            e = group(NJ - 1, False, True)
            routed_down(UNITS - 2, UNITS % 2, e[QU - 2])
            hid_t(UNITS - 1 + N0, (UNITS - 1) % 2)
            routed_down(UNITS - 1, (UNITS - 1) % 2, e[QU - 1])

        @block.scalar
        def _(act):
            A = nc.scalar.activation

            def xnT_of(f):
                for i in range(2):
                    act.wait_ge(xnT_ps, of(f, 2, i + 1))
                    A(xnT[:, i * 512:(i + 1) * 512], bank_t[i][:, :], ACT.Copy).then_inc(xnT_sb, 1)

            def exps(f):
                for i in range(2):
                    act.wait_ge(q_ps, of(f, 2, i + 1))
                    A(q_e[:, i, :], bank_p[i][:, :], ACT.Exp, bias=minus1[:, 0:1]).then_inc(q_exp, 1)
                for i in range(4):
                    act.wait_ge(kv_ps, of(f, 4, i + 1))
                    o = bank_p[i % 2][:, :].rearrange("p (h n) -> p h n", h=2)
                    A(v1[:, 2 * i:2 * i + 2, 0:E], o[:, :, E:2 * E], ACT.Copy)
                    A(k_e[:, i % 2, :, :], o[:, :, 0:E], ACT.Exp, bias=minus1[:, 0:1]).then_inc(kv_exp, 1)

            def silu_of(n_, i):
                act.wait_ge(gu_ps, n_ + 1)
                A(act_g[:, i, :], bank_g[i][:, 0:INTER], ACT.Silu).then_inc(silu, 1)

            def ht_of(n_, i):
                act.wait_ge(ht_ps, n_ + 1)
                A(hidT[:, i, :], bank_h[i][:, 0:INTER], ACT.Copy).then_inc(ht_sb, 1)

            def u_of(k, par):
                act.wait_ge(u_norm, of(k, 1, 1))
                for t in range(NT // 2, NT):
                    ins = A(u_row[par][:, t, 0:E], kept(k, t * E, (t + 1) * E), ACT.Identity, bias=nb_u[:, t:t + 1], scale=r_u[:, t:t + 1])
                ins.then_inc(u_act, 1)

            def xn_of(f, par):
                act.wait_ge(x_norm, of(f, 1, 1))
                for t in range(XN_DVE, NT):
                    ins = A(xn[:, t, :], xin[par][:, t, :], ACT.Identity, bias=nb_x[:, t:t + 1], scale=r_ax[:, NT + t:NT + t + 1])
                ins.then_inc(xn_act, 1)

            def router_exp(m):
                act.wait_ge(r_ready, of(m, 1, 1))
                A(r_exp[:, :, :], r_in[:, :, :], ACT.Exp).then_inc(r_done, 1)

            def uT_of(k, i):
                act.wait_ge(uT_ps, of(k, 2, i + 1))
                A(uT_at(k)[:, i * 512:(i + 1) * 512], bank_t[1 - i][:, :], ACT.Copy).then_inc(uT_sb, 1)

            def step(s, par):
                if has(s - 2) and not late(s - 2):
                    router_exp(s - 2)
                if has(s):
                    exps(s)
                k = s - 1
                if is_int(s) and s == B:
                    late_units(0, LATE_EARLY)
                if has(k):
                    u_of(k, 1 - par)
                    uT_of(k, 0)
                if is_int(k) and k == B - 1:
                    uT_of(k, 1)
                    router_exp(k)
                    late_units(LATE_EARLY, LATE * NT + 2)
                    return
                own = has(k) and not late(k)
                for t in range(NT + 2):
                    n_ = k * NT + t
                    if own and t < NT:
                        silu_of(n_, t % 2)
                    if has(k) and t == 1:
                        uT_of(k, 1)
                        if late(k):
                            router_exp(k)
                    if own and t >= 2:
                        shared_y(n_ - 2, k, t - 2)
                    if own and 1 <= t <= NT:
                        ht_of(n_ - 1, (t - 1) % 2)
                    if has(s + 1) and t == XN_AT:
                        xn_of(s + 1, 1 - par)
                    if has(s + 1) and t == XNT_AT:
                        xnT_of(s + 1)

            def shared_y(n_, b, t):
                act.wait_ge(y_ps, n_ + 1)
                A(kept(b, (NT + t) * E, (NT + t + 1) * E), bank_h[t % 2][:, INTER:INTER + E], ACT.Copy).then_inc(y_sb, 1)

            def late_units(a, z):
                for i in range(a, z):
                    n_ = (B - LATE) * NT + i
                    if i < LATE * NT:
                        silu_of(n_, i % 2)
                    if i >= 2:
                        shared_y(n_ - 2, (n_ - 2) // NT, (n_ - 2) % NT)
                    if 1 <= i <= LATE * NT:
                        ht_of(n_ - 1, (i - 1) % 2)

            act.wait_ge(setup_ps, 3)
            xn_of(0, 0)
            xnT_of(0)
            schedule(act, step)

            N0 = TOK // P

            def x_hi(n_, i):
                act.wait_ge(xbT_ps, n_ + 1)
                A(xbT[0][:, i, :], bank_t[i][:, 0:E], ACT.Copy).then_inc(xbT_hi, 1)

            def y_of(n_, i, j, first):
                act.wait_ge(y_ps, n_ + N0 + 1)
                if not first:
                    act.wait_ge(y_out[i // HALF], (j - (1 if i >= QU - 2 else 0)) * 16 * HALF)
                A(yb[:, i, :], bank_h[i % 2][:, INTER:INTER + E], ACT.Copy, scale=yw[:, i:i + 1]).then_inc(y_sb, 1)

            def unit(j, i, first, y_first):
                n_ = j * QU + i
                x_hi(n_ + 1, (i + 1) % 2)
                silu_of(n_ + N0, i % 2)
                if not first or i >= 2:
                    y_of(n_ - 2, (i - 2) % QU, j, y_first)
                if not first or i >= 1:
                    ht_of(n_ + N0 - 1, (i - 1) % 2)

            x_hi(0, 0)
            for i in range(QU):
                unit(0, i, True, True)
            for i in range(QU):
                unit(1, i, False, i < 2)
            with act.Fori(2, GROUPS - 1) as j:
                for i in range(QU):
                    unit(j, i, False, False)
            J = GROUPS - 1
            for i in range(QU - 1):
                unit(J, i, False, False)
            silu_of(UNITS - 1 + N0, (UNITS - 1) % 2)
            y_of(UNITS - 3, (UNITS - 3) % QU, J, False)
            ht_of(UNITS - 2 + N0, (UNITS - 2) % 2)
            y_of(UNITS - 2, (UNITS - 2) % QU, J + 1, False)
            ht_of(UNITS - 1 + N0, (UNITS - 1) % 2)
            y_of(UNITS - 1, (UNITS - 1) % QU, J + 1, False)

            for g, (first, batches, act_tiles) in enumerate(C_GROUPS):
                act.wait_ge(rc_ready, g + 1)
                for h in range(batches):
                    for t in range(act_tiles):
                        y = kept(first + h, (NT + t) * E, (NT + t + 1) * E)
                        at = slice(h * NT + t, h * NT + t + 1)
                        ins = A(y, y, ACT.Identity, bias=shift[:, g % 2, at], scale=r_c[:, g % 2, at])
                    ins.then_inc(y_normed, 1)

        @block.vector
        def _(dv):
            v = nc.vector
            base, n = [0], [0]

            def inc(ins):
                n[0] += 1
                ins.then_inc(dve, 1)
                return n[0]

            def wait(k=None):
                dv.wait_ge(dve, base[0] + (n[0] if k is None else k))

            def link(ins):
                inc(ins)
                wait()

            def rsqrt(dst, var, t):
                k = inc(v.tensor_scalar(dst.bitcast(i32), var.bitcast(i32), -0.5, float(0x5f3759df), ALU.mult, ALU.add))
                yield
                for _ in range(3):
                    wait(k)
                    k = inc(v.tensor_tensor(t, dst, dst, ALU.mult))
                    yield
                    wait(k)
                    k = inc(v.scalar_tensor_tensor(out=t, in0=t, scalar=-0.5, in1=var, op0=ALU.mult, op1=ALU.mult))
                    yield
                    wait(k)
                    k = inc(v.scalar_tensor_tensor(out=dst, in0=t, scalar=1.5, in1=dst, op0=ALU.add, op1=ALU.mult))
                    yield
                wait(k)

            def stats(src, st, mv, ve, tiles=NT):
                for t in range(tiles):
                    k = inc(v.bn_stats(st[:, t, :], src(t)))
                    yield
                wait(k)
                dv.sem_inc(dve_passed, 1)
                for t in range(tiles):
                    k = inc(v.bn_aggr(mv[:, t, :], st[:, t, :]))
                    yield
                wait(k)
                k = inc(v.tensor_scalar(ve, mv[:, 0:tiles, 1], LN_EPS, None, ALU.add))
                yield
                wait(k)

            minus_one = v.memset(minus1[:, :], -1.0)
            inc(minus_one)
            link(v.memset(bias_acc[:, :], 0.0))
            link(v.memset(bias_bf[:, :], 0.0))
            def weights_setup():
                dv.wait_ge(consts, 1)
                dv.wait_ge(w_loaded, 16 * 7)
                inc(v.tensor_scalar(gate_s[:, :], gate_t[:, :], ln_sc[:, 0:1], None, ALU.mult))
                v.tensor_scalar(ln_bi_w[:, :], ones[:, :], ln_bi[:, 0:1], None, ALU.mult).then_inc(setup_ps, 1)
                c = inc(v.tensor_scalar(bias3[0:3, 0:2 * E], bias3[0:3, 0:2 * E], 1.0, None, ALU.add))
                yield
                for i in range(3):
                    wait(c)
                    c = inc(v.tensor_copy(bias_part[0:3, :], bias3[0:3, :]))
                    yield
                    wait(c)
                    c = inc(v.scalar_tensor_tensor(out=bias_acc[0:3, :], in0=bias_part[0:3, :], scalar=ident[0:3, i:i + 1], in1=bias_acc[0:3, :], op0=ALU.mult, op1=ALU.add))
                    yield
                    if i < 2:
                        c = inc(v.tensor_tensor(bias3[0:3, :], bias3[0:3, :], bias_part[0:3, :], ALU.subtract))
                        yield
                wait(c)
                v.tensor_copy(bias_bf[0:3, :], bias_acc[0:3, :])
                dv.wait_ge(setup_ps, 2)
                v.tensor_copy(gate_b[:, :], bank_h[0][:, NE:2 * NE])
                v.scalar_tensor_tensor(out=gate_c[:, :], in0=bank_h[0][:, 0:NE], scalar=-1.0 / E, in1=gate_s[:, :], op0=ALU.mult, op1=ALU.add).then_inc(setup_ps, 1)
                yield

            def phi(f):
                for i in range(2):
                    dv.wait_ge(q_exp, of(f, 2, i + 1))
                    v.scalar_tensor_tensor(out=pqT[:, i * 512:(i + 1) * 512], in0=q_e[:, i, :], scalar=1.0, in1=bank_p[i][:, :],
                                           op0=ALU.min, op1=ALU.max).then_inc(pq_sb, 1)
                    yield
                for i in range(4):
                    dv.wait_ge(kv_exp, of(f, 4, i + 1))
                    v.scalar_tensor_tensor(out=pk[:, 2 * i:2 * i + 2, :], in0=k_e[:, i % 2, :, :], scalar=1.0,
                                           in1=bank_p[i % 2][:, :].rearrange("p (h n) -> p h n", h=2)[:, :, 0:E],
                                           op0=ALU.min, op1=ALU.max).then_inc(pk_sb, 1)
                    yield
                dv.wait_ge(sum_ps, of(f, 1, 1))
                v.tensor_tensor(kvm[:, 0:E].rearrange("p (h m) -> p h m", m=D), bank_t[0][:, 0:E].rearrange("p (h m) -> p h m", m=D),
                                head_mask[:, :].unsqueeze(2).to_broadcast([P, HEADS, D]), ALU.mult)
                v.tensor_scalar(kvm[:, E:E + HEADS], head_mask[:, :], bank_t[0][:, E:E + 1], None, ALU.mult).then_inc(kvm_sb, 1)
                yield

            def hidden(n_, i):
                dv.wait_ge(silu, n_ + 1)
                v.tensor_tensor(hid[:, i, :], act_g[:, i, :], bank_g[i][:, INTER:2 * INTER], ALU.mult).then_inc(hid_sb, 1)

            def products(m):
                for t in range(NT):
                    hidden(m * NT + t, t % 2)
                    yield

            def attention(f):
                for i in range(4):
                    dv.wait_ge(attn_ps, of(f, 4, i + 1))
                    a = bank_p[i % 2][:, :].rearrange("p (h n) -> p h n", h=2)
                    c = inc(v.tensor_scalar(zt[:, i % 2, :, :], a[:, :, E:E + HEADS], 1e-6, None, ALU.add))
                    yield
                    wait(c)
                    c = inc(v.reciprocal(zr[:, i % 2, :, :], zt[:, i % 2, :, :]))
                    yield
                    wait(c)
                    for h in range(2):
                        last = v.tensor_tensor(att[:, 2 * i + h, :].rearrange("p (h m) -> p h m", m=D), a[:, h, 0:E].rearrange("p (h m) -> p h m", m=D),
                                               zr[:, i % 2, h, :].unsqueeze(2).to_broadcast([P, HEADS, D]), ALU.mult)
                    last.then_inc(att_sb, 1)
                    yield
                dv.wait_ge(att_sb, of(f, 4, 4))

            def residual(k, par):
                x1 = kept(k, 0, NT * E).rearrange("p (t n) -> p t n", n=E)
                for t in range(NT):
                    last = v.scalar_tensor_tensor(out=x1[:, t, :], in0=att[:, t, :], scalar=r_ax[:, t:t + 1], in1=xin[par][:, t, :], op0=ALU.mult, op1=ALU.add)
                    if t < NT - 1:
                        yield
                last.then_inc(x1_done, 1)
                v.scalar_tensor_tensor(out=kept(k, 2 * NT * E, KEEP), in0=mv_a[:, :, 0], scalar=-1.0, in1=r_ax[:, 0:NT], op0=ALU.mult, op1=ALU.mult)
                yield
                dv.wait_ge(x1_done, of(k, 1, 1))
                dv.sem_inc(dve_passed, 1)
                yield from stats(lambda t: x1[:, t, :], st_a, mv_u, ve_u[:, :])
                yield from rsqrt(r_u[:, :], ve_u[:, :], nt_u[:, :])
                if is_int(k) and k == 1:
                    dv.wait_ge(spare_in, 16)
                    dv.wait_ge(w_split, 4)
                if not is_int(k) or k >= 2:
                    dv.wait_ge(scattered[par], (k - par) * (8 * 2 * NT))
                v.scalar_tensor_tensor(out=nb_u[:, :], in0=mv_u[:, :, 0], scalar=-1.0, in1=r_u[:, :], op0=ALU.mult, op1=ALU.mult).then_inc(u_norm, 1)
                yield
                for t in range(NT // 2):
                    last = v.tensor_scalar(u_row[par][:, t, 0:E], x1[:, t, :], mv_u[:, t, 0:1], r_u[:, t:t + 1], ALU.subtract, ALU.mult)
                    if t < NT // 2 - 1:
                        yield
                last.then_inc(u_dve, 1)
                yield

            def norms(f, g, par):
                if has(f):
                    yield from stats(lambda t: att[:, t, :], st_a, mv_a, ve[:, 0:NT])
                if has(g):
                    dv.wait_ge(x_loaded[par], (g - par) * 8 + 16)
                    yield from stats(lambda t: xin[par][:, t, :], st_1, mv_1, ve[:, NT:2 * NT])
                cols = slice(0 if has(f) else NT, 2 * NT if has(g) else NT)
                yield from rsqrt(r_ax[:, cols], ve[:, cols], nt_[:, cols])
                if has(g):
                    v.scalar_tensor_tensor(out=nb_x[:, :], in0=mv_1[:, :, 0], scalar=-1.0, in1=r_ax[:, NT:2 * NT], op0=ALU.mult, op1=ALU.mult).then_inc(x_norm, 1)
                    yield
                    for t in range(XN_DVE):
                        last = v.tensor_scalar(xn[:, t, :], xin[par][:, t, :], mv_1[:, t, 0:1], r_ax[:, NT + t:NT + t + 1], ALU.subtract, ALU.mult)
                        if t < XN_DVE - 1:
                            yield
                    last.then_inc(xn_dve, 1)
                    yield

            def bc(a):
                return a.unsqueeze(2).to_broadcast([P, NT, NE])

            def per_e(a):
                return a.unsqueeze(1).to_broadcast([P, NT, NE])

            total_at = [0]

            def router(m, par):
                c = inc(v.tensor_tensor(ve_4[:, :], mv_u[:, :, 1], r_u[:, :], ALU.mult))
                yield
                wait(c)
                c = inc(v.tensor_tensor(ve_4[:, :], ve_4[:, :], r_u[:, :], ALU.mult))
                yield
                wait(c)
                c = inc(v.tensor_scalar(ve_4[:, :], ve_4[:, :], LN_EPS, None, ALU.add))
                yield
                wait(c)
                yield from rsqrt(r_4[:, :], ve_4[:, :], nt_4[:, :])
                dv.wait_ge(logit_ps, of(m, 1, 1))
                c = inc(v.tensor_tensor(lg[:, :, :], bank_t[1][:, 0:NT * NE].rearrange("p (t e) -> p t e", e=NE), bc(r_4[:, :]), ALU.mult))
                yield
                wait(c)
                v.tensor_tensor(lg[:, :, :], lg[:, :, :], per_e(gate_b[:, :]), ALU.add).then_inc(logit_read, 1)
                yield
                dv.wait_ge(logit_read, of(m, 1, 1))
                c = inc(v.tensor_reduce(m1[:, :], lg[:, :, :], AX.X, ALU.max))
                yield
                wait(c)
                c = inc(v.tensor_tensor(cand[:, :, :], lg[:, :, :], bc(m1[:, :]), ALU.is_equal))
                yield
                wait(c)
                c = inc(v.tensor_tensor(cand[:, :, :], cand[:, :, :], per_e(rank_of[:, :]), ALU.mult))
                yield
                wait(c)
                c = inc(v.tensor_reduce(i1[:, :], cand[:, :, :], AX.X, ALU.max))
                yield
                wait(c)
                c = inc(v.tensor_tensor(oh1[:, :, :], per_e(rank_of[:, :]), bc(i1[:, :]), ALU.is_equal))
                yield
                wait(c)
                c = inc(v.scalar_tensor_tensor(out=lg2[:, :, :], in0=oh1[:, :, :], scalar=-3e38, in1=lg[:, :, :], op0=ALU.mult, op1=ALU.add))
                yield
                wait(c)
                c = inc(v.tensor_reduce(m2[:, :], lg2[:, :, :], AX.X, ALU.max))
                yield
                wait(c)
                v.tensor_tensor(r_in[:, :, 0:NE], lg[:, :, :], bc(m1[:, :]), ALU.subtract)
                v.tensor_tensor(r_in[:, :, NE], m2[:, :], m1[:, :], ALU.subtract).then_inc(r_ready, 1)
                yield
                c = inc(v.tensor_tensor(cand[:, :, :], lg2[:, :, :], bc(m2[:, :]), ALU.is_equal))
                yield
                wait(c)
                c = inc(v.tensor_tensor(cand[:, :, :], cand[:, :, :], per_e(rank_of[:, :]), ALU.mult))
                yield
                wait(c)
                c = inc(v.tensor_reduce(i2[:, :], cand[:, :, :], AX.X, ALU.max))
                yield
                wait(c)
                c = inc(v.tensor_tensor(oh2[:, :, :], per_e(rank_of[:, :]), bc(i2[:, :]), ALU.is_equal))
                yield
                wait(c)
                v.tensor_tensor(oh_bf[:, :, :], oh1[:, :, :], oh2[:, :, :], ALU.add).then_inc(oh_ready, 1)
                yield
                v.tensor_scalar(u_row[par][:, :, E + 1], i1[:, :], -1.0, float(NE), ALU.mult, ALU.add)
                v.tensor_copy(u_row[par][:, :, E], tok2[:, ds(m * NT, NT)])
                yield
                dv.wait_ge(oh_ready, of(m, 1, 1))
                total_at[0] = inc(v.tensor_reduce(total_new[:, :], oh_bf[:, :, :].rearrange("p t e -> p e t"), AX.X, ALU.add))
                yield

            def weights(m, par):
                dv.wait_ge(r_done, of(m, 1, 1))
                c = inc(v.tensor_reduce(esum[:, :], r_exp[:, :, 0:NE], AX.X, ALU.add))
                yield
                wait(c)
                c = inc(v.scalar_tensor_tensor(out=den[:, :], in0=esum[:, :], scalar=EPS, in1=r_exp[:, :, NE], op0=ALU.mult, op1=ALU.add))
                yield
                wait(c)
                c = inc(v.tensor_scalar(den[:, :], den[:, :], 1.0, None, ALU.add))
                yield
                wait(c)
                c = inc(v.reciprocal(wden[:, :], den[:, :]))
                yield
                wait(c)
                v.tensor_copy(u_row[par][:, :, E + 2], wden[:, :])
                yield
                v.scalar_tensor_tensor(out=u_row[par][:, :, E + 3], in0=r_exp[:, :, NE], scalar=-1.0, in1=wden[:, :], op0=ALU.add, op1=ALU.mult).then_inc(slots_ready, 1)
                yield

            def slots(m, par):
                dv.wait_ge(rank_ps, of(m, 1, 1))
                wait(total_at[0])
                v.tensor_tensor(pos[:, :, :], bank_t[1][:, 64:128].rearrange("p (t e) -> p t e", e=NE), per_e(region[:, :]), ALU.add).then_inc(rank_read, 1)
                c = inc(v.tensor_tensor(total[:, :], total[:, :], total_new[:, :], ALU.add))
                yield
                wait(c)
                inc(v.tensor_copy(total_bf[:, :], total[:, :]))
                inc(v.tensor_tensor(oh1[:, :, :], oh1[:, :, :], pos[:, :, :], ALU.mult))
                c = inc(v.tensor_tensor(oh2[:, :, :], oh2[:, :, :], pos[:, :, :], ALU.mult))
                yield
                wait(c)
                inc(v.tensor_reduce(slot_f[:, 0:NT], oh1[:, :, :], AX.X, ALU.add))
                c = inc(v.tensor_reduce(slot_f[:, NT:2 * NT], oh2[:, :, :], AX.X, ALU.add))
                yield
                wait(c)
                inc(v.tensor_copy(slot_i[par][:, :], slot_f[:, :]))
                yield

            def main(s, par):
                if has(s - 1):
                    yield from residual(s - 1, 1 - par)
                if has(s):
                    yield from attention(s)
                    yield from norms(s, s + 1, 1 - par)

            def nothing():
                return iter(())

            def table():
                dv.wait_ge(cnt_ps, 1)
                c = inc(v.tensor_copy(cnt[:, :], bank_t[0][:, 0:NE]))
                yield
                wait(c)
                inc(v.tensor_tensor(pad_f[:, :], cnt[:, :], region[:, :], ALU.add))
                c = inc(v.tensor_scalar(tl_i[:, :], cnt[:, :], float(P - 1), None, ALU.add))
                yield
                wait(c)
                c = inc(v.tensor_scalar(tl_s[:, :], tl_i[:, :], 7, None, ALU.arith_shift_right))
                yield
                wait(c)
                v.tensor_copy(pad_i[:, :], pad_f[:, :]).then_inc(pads_ready, 1)
                c = inc(v.tensor_copy(tl[:, :], tl_s[:, :]))
                yield
                wait(c)
                inc(v.tensor_scalar(gain[:, :], tl[:, :], float(-P), float(CAP + (1 << SHIFT)), ALU.mult, ALU.add))
                c = inc(v.tensor_tensor(tl8[:, :, :], lower8[:, :, :], tl[:, :].unsqueeze(1).to_broadcast([P, NE, NE]), ALU.mult))
                yield
                wait(c)
                c = inc(v.tensor_reduce(cum[:, :], tl8[:, :, :], AX.X, ALU.add))
                yield
                wait(c)
                c = inc(v.tensor_tensor(past[:, :, :], unit_no[:, :].unsqueeze(2).to_broadcast([P, UNITS, NE]),
                                     cum[:, :].unsqueeze(1).to_broadcast([P, UNITS, NE]), ALU.is_ge))
                yield
                wait(c)
                c = inc(v.tensor_tensor(past[:, :, :], past[:, :, :], gain[:, :].unsqueeze(1).to_broadcast([P, UNITS, NE]), ALU.mult))
                yield
                wait(c)
                c = inc(v.tensor_reduce(pk_sum[:, :], past[:, :, :], AX.X, ALU.add))
                yield
                wait(c)
                c = inc(v.scalar_tensor_tensor(out=pk_i[:, :], in0=unit_no[:, :], scalar=float(P), in1=pk_sum[:, :], op0=ALU.mult, op1=ALU.add))
                yield
                wait(c)
                inc(v.tensor_scalar(unit_row[:, :], pk_i[:, :], (1 << SHIFT) - 1, None, ALU.bitwise_and))
                c = inc(v.tensor_scalar(unit_w[:, :], pk_i[:, :], SHIFT, None, ALU.arith_shift_right))
                yield
                wait(c)
                inc(v.tensor_copy(unit_ef[:, :], unit_w[:, :]))
                c = inc(v.tensor_scalar(unit_e[:, 2:2 + UNITS], unit_w[:, :], float(NE - 1), None, ALU.min))
                yield
                wait(c)
                c = inc(v.tensor_tensor(own_terms[:, :, :], unit_e[:, 2:2 + UNITS].rearrange("p (g u) -> p g u", u=QU), powers[:, :].unsqueeze(1).to_broadcast([P, GROUPS, QU]), ALU.mult))
                yield
                wait(c)
                inc(v.tensor_reduce(own_f[:, :], own_terms[:, :, :], AX.X, ALU.add))
                before = unit_e[:, 0:UNITS].rearrange("p (g u) -> p g u", u=QU)
                c = inc(v.scalar_tensor_tensor(out=before_i[:, :], in0=before[:, :, 1], scalar=float(NE), in1=before[:, :, 0], op0=ALU.mult, op1=ALU.add))
                yield
                wait(c)
                inc(v.tensor_copy(own_i[:, :], own_f[:, :]))
                c = inc(v.tensor_scalar(before_i[:, :], before_i[:, :], 3 * QU, None, ALU.logical_shift_left))
                yield
                wait(c)
                v.tensor_tensor(unit_pack[:, :], own_i[:, :], before_i[:, :], ALU.bitwise_or).then_inc(table_ready, 1)
                wait()

            def final_step(m, par):
                shared = (0 for b in range(B - LATE, B) for _ in products(b))
                for i, _ in enumerate(residual(m, par)):
                    if i in LATE_EARLY_AT:
                        next(shared)
                for _ in router(m, par):
                    pass
                tail = weights(m, par)
                for _ in range(5):
                    next(tail)
                for strand in (slots(m, par), tail):
                    for _ in strand:
                        pass
                dv.wait_ge(slots_ready, B)
                v.tensor_copy(total_bf[:, :], total[:, :]).then_inc(oh_ready, 1)
                units = table()
                for i, _ in enumerate(shared, LATE_EARLY):
                    if i >= COUNT_AT:
                        for _ in range(TABLE_AT):
                            next(units, None)
                for _ in units:
                    pass

            def step(s, par):
                if is_int(s) and s == B:
                    final_step(s - 1, 1 - par)
                    return
                side = [(phi(s) if has(s) else nothing(), PHI_AT),
                        (weights(s - 2, par) if has(s - 2) and not late(s - 2) else nothing(), WEIGHTS_AT),
                        (router(s - 1, 1 - par) if has(s - 1) else nothing(), ROUTER_AT),
                        (products(s - 1) if has(s - 1) and not late(s - 1) else nothing(), PRODUCTS_AT),
                        (slots(s - 1, 1 - par) if has(s - 1) else nothing(), SLOTS_AT)]
                if is_int(s) and s == 0:
                    for _ in side[0][0]:
                        pass
                for i, _ in enumerate(main(s, par)):
                    for strand, at in side:
                        if i in at:
                            next(strand, None)
                if has(s - 1) and late(s - 1):
                    side.append((weights(s - 1, 1 - par), ()))
                for strand, _ in side:
                    for _ in strand:
                        pass

            setup_strand = weights_setup()
            for i, _ in enumerate(norms(-1, 0, 0)):
                if i in SETUP_AT:
                    next(setup_strand, None)
            for _ in setup_strand:
                pass
            for s in range(3):
                step(s, s % 2)
            start = base[0] + n[0]
            LOOPS = (B - 4) // 2
            with dv.Fori(0, LOOPS) as j:
                base[0], n[0] = j * DVE_PAIR + start, 0
                step(j * 2 + 3, 1)
                step(j * 2 + 4, 0)
                assert n[0] == DVE_PAIR, f"DVE_PAIR = {n[0]}"
            base[0], n[0] = start + LOOPS * DVE_PAIR, 0
            for s in range(B - 1, B + 2):
                step(s, s % 2)
            N0 = TOK // P

            def x_lo(n_, i):
                dv.wait_ge(xbT_hi, n_ + 1)
                v.tensor_tensor(xbT[1][:, i, :], bank_t[i][:, 0:E], xbT[0][:, i, :].bitcast(f32), ALU.subtract).then_inc(xbT_lo, 1)

            def tails(j, h, first):
                u = slice(h * HALF, (h + 1) * HALF)
                dv.wait_ge(xb_in[h], j * 16 * HALF + 16 * HALF)
                if not first:
                    dv.wait_ge(y_out[h], j * 16 * HALF)
                c = inc(v.tensor_tensor(other[:, u], xb[:, u, E + 1], unit_ef[:, ds(j * QU + h * HALF, HALF)], ALU.not_equal))
                yield
                wait(c)
                c = inc(v.tensor_tensor(yw[:, u], other[:, u], xb[:, u, E + 3], ALU.mult))
                yield
                wait(c)
                inc(v.tensor_tensor(yi[:, u], other[:, u], xb[:, u, E], ALU.add))
                c = inc(v.tensor_tensor(yw[:, u], yw[:, u], xb[:, u, E + 2], ALU.add))
                yield
                wait(c)
                dv.sem_inc(yi_sb, 1)
                yield

            def units(j, first, final):
                for i in range(QU):
                    n_ = j * QU + i
                    if i % HALF == 0:
                        t = tails(j, i // HALF, first)
                    next(t, None)
                    if not (final and i == QU - 1):
                        x_lo(n_ + 1, (i + 1) % 2)
                    next(t, None)
                    hidden(n_ + N0, i % 2)
                    if i % HALF == 0:
                        for _ in t:
                            pass

            dv.sem_inc(xbT_lo, N0 - 1)
            dv.wait_ge(xb_in[0], 16 * HALF)
            x_lo(0, 0)
            units(0, True, False)
            start = base[0] + n[0]
            with dv.Fori(1, GROUPS - 1) as j:
                base[0], n[0] = (j - 1) * (2 * 4) + start, 0
                units(j, False, False)
                assert n[0] == 2 * 4
            base[0], n[0] = start + (GROUPS - 2) * 2 * 4, 0
            units(GROUPS - 1, False, True)
            def c_stats(g):
                first, batches, _ = C_GROUPS[g]
                for b in range(first, first + batches):
                    dv.wait_ge(y1_in[b], 16)
                yield from stats(lambda t: kept(first + t // NT, (NT + t % NT) * E, (NT + t % NT + 1) * E), st_c, mv_c, ve[:, 0:batches * NT], batches * NT)

            def c_scale(g):
                first, batches, _ = C_GROUPS[g]
                n_t = batches * NT
                r, z = r_c[:, g % 2, 0:n_t], shift[:, g % 2, 0:n_t]
                yield from rsqrt(r, ve[:, 0:n_t], nt_[:, 0:n_t])
                c = inc(v.tensor_tensor(z, mv_c[:, 0:n_t, 0], r, ALU.mult))
                yield
                wait(c)
                z = z.rearrange("p (b t) -> p b t", b=batches)
                v.tensor_tensor(z, keep[:, first:first + batches, 2 * NT * E:KEEP], z, ALU.subtract).then_inc(rc_ready, 1)
                yield

            def c_norm(g):
                first, batches, act_tiles = C_GROUPS[g]
                dv.wait_ge(rc_ready, g + 1)
                for h in range(batches):
                    for t in range(act_tiles, NT):
                        y = kept(first + h, (NT + t) * E, (NT + t + 1) * E)
                        at = slice(h * NT + t, h * NT + t + 1)
                        inc(v.tensor_scalar(y, y, r_c[:, g % 2, at], shift[:, g % 2, at], ALU.mult, ALU.add))

            def c_add(g, k):
                first, batches, _ = C_GROUPS[g]
                for b in range(first, first + batches):
                    wait(k)
                    dv.wait_ge(y_normed, b + 1)
                    v.tensor_tensor(kept(b, 0, NT * E), kept(b, 0, NT * E), kept(b, NT * E, 2 * NT * E), ALU.add).then_inc(res_ready, 1)
                    yield

            normed = None
            for g in range(len(C_GROUPS)):
                for _ in c_stats(g):
                    pass
                if g >= 2:
                    dv.wait_ge(y_normed, C_GROUPS[g - 1][0])
                add = c_add(g - 1, normed) if g and C_GROUPS[g - 1][0] >= POOL_ADDS else iter(())
                for i, _ in enumerate(c_scale(g)):
                    if i in C_ADD_AT:
                        next(add, None)
                for _ in add:
                    pass
                c_norm(g)
                normed = n[0]
            for _ in c_add(len(C_GROUPS) - 1, normed):
                pass


_INS = ['L0_attn_x', 'L0_attn_W_qkv', 'L0_attn_b_qkv', 'L0_attn_W_proj', 'L0_attn_b_proj', 'L0_ffn_ln_scale',
        'L0_ffn_ln_bias', 'L0_ffn_gate_w', 'L0_ffn_Wg', 'L0_ffn_Wu', 'L0_ffn_Wd', 'L0_ffn_sWg', 'L0_ffn_sWu', 'L0_ffn_sWd']


def kernel(**inputs):
    import numpy as _np
    import concourse.bacc as _bacc
    from concourse import mybir as _mybir
    from concourse.bass_utils import run_bass_kernel_spmd as _run

    nc = _bacc.Bacc("TRN2", target_bir_lowering=False, num_devices=1)
    arrays, args = {}, []
    for name in _INS:
        a = _np.ascontiguousarray(inputs[name])
        arrays[f"in_{name}"] = a
        args.append(nc.dram_tensor(f"in_{name}", a.shape, _mybir.dt.from_np(a.dtype), kind="ExternalInput").ap())
    args.append(nc.dram_tensor("out_dram", (B, S, E), _mybir.dt.float32, kind="ExternalOutput").ap())
    program(nc, *args)
    r = _run(nc, [arrays], core_ids=[0])
    return r.results[0]["out_dram"]
```
